# Optimizing a Trainium2 kernel written in Bass

```python
import numpy as np
import jax
import jax.numpy as jnp

def _softmax(x, axis=-1):
    return jax.nn.softmax(x, axis=axis)

def _gelu(x):
    return jax.nn.gelu(x, approximate=True)

def _silu(x):
    return jax.nn.silu(x)

def _sigmoid(x):
    return jax.nn.sigmoid(x)

def _layernorm(x, axis=-1, eps=1e-05):
    m = jnp.mean(x, axis=axis, keepdims=True)
    v = jnp.var(x, axis=axis, keepdims=True)
    return (x - m) / jnp.sqrt(v + eps)

def _scatter_add(tgt, idx, src, axis=0):
    return tgt.at[idx].add(src)

def _segment_sum(src, seg, n):
    return jax.ops.segment_sum(src, seg, n)
kernel_name = 'mk_decoder_preln_d1_seqx_r4_23ee3c'

def setup_inputs(seed: int=0):
    np.random.seed(seed)
    _w = jnp.asarray

    def _rec_inputs():
        import jax
        import jax.numpy as jnp
        _rk = jax.random.key(seed)
        x = 7.22e-05 + 1 * jax.random.normal(jax.random.fold_in(_rk, 1), (4, 512, 512), jnp.float32)
        _lenS = 512 - jax.random.randint(jax.random.fold_in(_rk, 7), (4,), 0, max(1, 512 // 4) + 1, jnp.int32)
        _lenS2 = 512 - jax.random.randint(jax.random.fold_in(_rk, 8), (4,), 0, max(1, 512 // 4) + 1, jnp.int32)
        _ctx_512P = jax.random.normal(jax.random.fold_in(_rk, 11), (4, 16, 128), jnp.float32)
        _ctx_512c = jax.random.dirichlet(jax.random.fold_in(_rk, 511), 0.3 * jnp.ones((16,), jnp.float32), (4, 512))
        _ctx_512t = jnp.einsum('bsk,bkd->bsd', _ctx_512c, _ctx_512P)
        _ctx_512t = _ctx_512t * jax.lax.rsqrt(jnp.mean(jnp.square(_ctx_512t)) + 1e-12) * 0.953939
        ctx_512 = -0.000514642 + 1.00011 * (_ctx_512t + 0.3 * jax.random.normal(jax.random.fold_in(_rk, 611), (4, 512, 128), jnp.float32))
        return (x, ctx_512)
    x, ctx_512 = _rec_inputs()

    def _L0_attn_setup():
        import jax, jax.numpy as jnp
        import numpy as np
        B, S, HID = (1, 1024, 512)
        NH, NKV, D = (16, 4, 128)
        QPG = NH // NKV
        GROUP = (QPG + 2) * D
        TOTAL = NKV * GROUP
        key = jax.random.key(seed)
        k0, k1, k2 = jax.random.split(key, 3)
        x = jax.random.normal(k0, (B, S, HID), dtype=jnp.float32)
        weight_qkv = jax.random.normal(k1, (TOTAL, HID), dtype=jnp.float32) * 0.02
        weight_proj = jax.random.normal(k2, (HID, NH * D), dtype=jnp.float32) * 0.02
        return {'x': x, 'weight_qkv': weight_qkv, 'weight_proj': weight_proj}
    _L0_attn_all = _L0_attn_setup()
    _L0_attn_in = {k: v for k, v in _L0_attn_all.items() if k in ('weight_qkv', 'weight_proj')}
    del _L0_attn_all

    def _L0_xattn_setup():
        import jax, jax.numpy as jnp
        import numpy as np
        import math
        NUM_Q_HEADS = 32
        NUM_KV_HEADS = 8
        key = jax.random.key(seed)
        k1, k2, k3 = jax.random.split(key, 3)
        B, S, E = (2, 512, 512)
        kv_E = NUM_KV_HEADS * (E // NUM_Q_HEADS)
        q = jax.random.normal(k1, (B, S, E), dtype=jnp.float32)
        k = jax.random.normal(k2, (B, S, kv_E), dtype=jnp.float32)
        v = jax.random.normal(k3, (B, S, kv_E), dtype=jnp.float32)
        return {'q': q, 'k': k, 'v': v}
    _L0_xattn_all = _L0_xattn_setup()
    _L0_xattn_in = {k: v for k, v in _L0_xattn_all.items() if k in ()}
    del _L0_xattn_all

    def _L0_ffn_setup():
        import jax, jax.numpy as jnp
        import numpy as np
        E = 8
        K = 2
        C = 512
        I = 352
        IS = I * 2
        B, T = (2, 512)
        key = jax.random.key(seed)
        ks = jax.random.split(key, 9)
        s = 0.02
        return {'x': jax.random.normal(ks[0], (B, T, C), dtype=jnp.float32), 'gate_w': jax.random.normal(ks[1], (E, C), dtype=jnp.float32) * s, 'w1': jax.random.normal(ks[2], (E, I, C), dtype=jnp.float32) * s, 'w2': jax.random.normal(ks[3], (E, I, C), dtype=jnp.float32) * s, 'w3': jax.random.normal(ks[4], (E, C, I), dtype=jnp.float32) * s, 'sw1': jax.random.normal(ks[5], (IS, C), dtype=jnp.float32) * s, 'sw2': jax.random.normal(ks[6], (IS, C), dtype=jnp.float32) * s, 'sw3': jax.random.normal(ks[7], (C, IS), dtype=jnp.float32) * s}
    _L0_ffn_all = _L0_ffn_setup()
    _L0_ffn_in = {k: v for k, v in _L0_ffn_all.items() if k in ('gate_w', 'w1', 'w2', 'w3', 'sw1', 'sw2', 'sw3')}
    del _L0_ffn_all
    return {'x': x, 'ctx_512': ctx_512, 'L0_attn_weight_qkv': _L0_attn_in['weight_qkv'], 'L0_attn_weight_proj': _L0_attn_in['weight_proj'], 'L0_ffn_gate_w': _L0_ffn_in['gate_w'], 'L0_ffn_w1': _L0_ffn_in['w1'], 'L0_ffn_w2': _L0_ffn_in['w2'], 'L0_ffn_w3': _L0_ffn_in['w3'], 'L0_ffn_sw1': _L0_ffn_in['sw1'], 'L0_ffn_sw2': _L0_ffn_in['sw2'], 'L0_ffn_sw3': _L0_ffn_in['sw3']}

def reference(x, ctx_512, L0_attn_weight_qkv, L0_attn_weight_proj, L0_ffn_gate_w, L0_ffn_w1, L0_ffn_w2, L0_ffn_w3, L0_ffn_sw1, L0_ffn_sw2, L0_ffn_sw3):
    import jax
    import jax.numpy as jnp

    def _L0_attn_ref(x, weight_qkv, weight_proj):
        import jax, jax.numpy as jnp
        import numpy as np
        B, S, HID = (1, 1024, 512)
        NH, NKV, D = (16, 4, 128)
        QPG = NH // NKV
        GROUP = (QPG + 2) * D
        TOTAL = NKV * GROUP
        b, s, _ = x.shape
        qkv = jnp.einsum('bsh,ph->bsp', x, weight_qkv).reshape(b, s, NKV, GROUP)
        q = qkv[..., :QPG * D].reshape(b, s, NKV, QPG, D)
        k = qkv[..., QPG * D:(QPG + 1) * D]
        v = qkv[..., (QPG + 1) * D:]
        scale = 1.0 / jnp.sqrt(jnp.float32(D))
        scores = jnp.einsum('bsgqd,btgd->bgqst', q, k) * scale
        causal = jnp.tril(jnp.ones((s, s), dtype=bool))
        scores = jnp.where(causal, scores, jnp.finfo(scores.dtype).min)
        attn = jax.nn.softmax(scores, axis=-1)
        out = jnp.einsum('bgqst,btgd->bsgqd', attn, v)
        out = out.reshape(b, s, NH * D)
        return jnp.einsum('bse,he->bsh', out, weight_proj)

    def _L0_xattn_ref(q, k, v):
        import jax, jax.numpy as jnp
        import numpy as np
        import math
        NUM_Q_HEADS = 32
        NUM_KV_HEADS = 8
        B, S, E = q.shape
        H, KV = (NUM_Q_HEADS, NUM_KV_HEADS)
        D = E // H
        G = H // KV
        scale = math.sqrt(D)
        qh = q.reshape(B, S, KV, G, D).transpose(0, 2, 3, 1, 4)
        kh = k.reshape(B, S, KV, D).transpose(0, 2, 1, 3)
        vh = v.reshape(B, S, KV, D).transpose(0, 2, 1, 3)
        scores = jnp.einsum('bkgsd,bktd->bkgst', qh, kh) / scale
        weights = jax.nn.softmax(scores, axis=-1)
        out = jnp.einsum('bkgst,bktd->bkgsd', weights, vh)
        return out.transpose(0, 3, 1, 2, 4).reshape(B, S, E)

    def _L0_ffn_ref(x, gate_w, w1, w2, w3, sw1, sw2, sw3):
        import jax, jax.numpy as jnp
        import numpy as np
        E = 8
        K = 2
        C = 512
        I = 352
        IS = I * 2
        B, T = (2, 512)
        Bq, Tq, Cq = x.shape
        xf = x.reshape(-1, Cq)
        logits = xf @ gate_w.T
        probs = jax.nn.softmax(logits.astype(jnp.float32), axis=-1)
        topk_p, topk_i = jax.lax.top_k(probs, K)
        comb = (jax.nn.one_hot(topk_i, E, dtype=jnp.float32) * topk_p[..., None]).sum(axis=1).astype(x.dtype)
        h1 = jnp.einsum('nc,eic->eni', xf, w1)
        h2 = jnp.einsum('nc,eic->eni', xf, w2)
        h = jax.nn.silu(h1) * h2
        eo = jnp.einsum('eni,eci->enc', h, w3)
        y = jnp.einsum('enc,ne->nc', eo, comb).reshape(Bq, Tq, Cq)
        sh = jax.nn.silu(xf @ sw1.T) * (xf @ sw2.T) @ sw3.T
        return y + sh.reshape(Bq, Tq, Cq)
    x = x + _L0_attn_ref(_layernorm(x, axis=-1), L0_attn_weight_qkv, L0_attn_weight_proj)
    x = x + _L0_xattn_ref(_layernorm(x, axis=-1), ctx_512, ctx_512)
    x = x + _L0_ffn_ref(_layernorm(x, axis=-1), L0_ffn_gate_w, L0_ffn_w1, L0_ffn_w2, L0_ffn_w3, L0_ffn_sw1, L0_ffn_sw2, L0_ffn_sw3)
    return x

_drawn_inputs = setup_inputs


def setup_inputs(seed=0):
    import zlib

    import numpy as np

    out = dict(_drawn_inputs(seed))
    spreads = {}
    factors = {'L0_ffn_gate_w': 7.285,
     'L0_ffn_w1': 6.287,
     'L0_ffn_w2': 6.159,
     'L0_ffn_w3': 6.161,
     'L0_ffn_sw1': 8.0,
     'L0_ffn_sw2': 8.0,
     'L0_ffn_sw3': 8.0}
    for name, (base, spread) in spreads.items():
        noise = np.random.default_rng([zlib.crc32(name.encode()), seed]).standard_normal(out[name].shape)
        drawn = base * np.exp(spread * noise) if base else spread * noise
        out[name] = jnp.asarray(drawn.astype(out[name].dtype))
    for name, factor in factors.items():
        out[name] = (out[name] * factor).astype(out[name].dtype)
    return out
```

```python
from contextlib import ExitStack

import concourse.bass as bass
from concourse import mybir

P = 128
ALU = mybir.AluOpType
ACT = mybir.ActivationFunctionType
AX_X = mybir.AxisListType.X
F32 = mybir.dt.float32
F32R = mybir.dt.float32r
BF16 = mybir.dt.bfloat16

BATCH, SEQ, HID = 4, 512, 512
TOK_TILES = SEQ // P
TILES = BATCH * TOK_TILES
KC = HID // P
GROUPS, QPG, D = 4, 4, 128
NPROJ = QPG + 2
EPS = 1e-5
MASKED = -3.0e38
ATT_SCALE = float(D) ** -0.5

PROJ_ORDER = [QPG, QPG + 1, 0, 1, 2, 3]
UNITS = QPG * TOK_TILES
PHASES = "ABC"


class Count:

    def __init__(self, sem, start=0):
        self.sem, self.start, self.n = sem, start, 0

    def mark(self, ins):
        ins.then_inc(self.sem, 1)
        self.n += 1
        return self.start + self.n

    def seal(self, eng, ins):
        eng.wait_ge(self.sem, self.mark(ins))

def side_work(b, last):
    plan = {6: ["k"], 7: ["v"], 8: ["q0"], 9: ["vt"], 10: ["q1"], 12: ["q2"], 14: ["q3"]}
    if b == BATCH - 1:
        if last:
            plan = {}
        else:
            plan[16], plan[17] = plan.pop(12), plan.pop(14)
        plan[18] = ["y0", "y1", "y2", "y3"]
    if b > 0:
        plan[2], plan[3], plan[4] = ["y0"], ["y1"], ["y2", "y3"]
    return plan


def attention_steps(last):
    ops = []
    for b in range(BATCH):
        plan = side_work(b, last)
        for s in range(UNITS + (3 if b == BATCH - 1 else 0)):
            score, done = b * UNITS + s + 1, b * UNITS + s - 1
            if s < UNITS and score < BATCH * UNITS + (not last):
                ops.append(("score", score))
            if b == 0 and s < QPG:
                ops.append(("split_out", s))
            if b == BATCH - 1 and s < NPROJ and not last:
                ops.append(("split_in", s))
            ops += [("chain", c, (b + 1) % BATCH) for c in plan.get(s, []) if c[0] != "y"]
            if s <= UNITS + 1 and done >= TOK_TILES and done % TOK_TILES == 0:
                ops.append(("pv", done // TOK_TILES - 1))
            if s <= UNITS and done >= 0:
                ops.append(("turn", done))
            ops += [("out", int(c[1]), b if s > UNITS else b - 1) for c in plan.get(s, []) if c[0] == "y"]
    return ops


def is_chain(op):
    return op[0] == "out" or (op[0] == "chain" and op[1] != "vt")


def is_turn(op):
    return op[0] == "turn" or (op[0] == "chain" and op[1] == "vt")


STEPS = {last: attention_steps(last) for last in (False, True)}
N_CHAIN = sum(map(is_chain, STEPS[False]))
N_TURN = sum(map(is_turn, STEPS[False]))
N_UNIT, N_HEAD, N_QKV, N_SPLIT = BATCH * UNITS, BATCH * QPG, BATCH * NPROJ, NPROJ + QPG
assert N_CHAIN % 2 == 0 and N_TURN % 2 == 0 and N_HEAD % 2 == 0


def walk(last):
    c = t = k = 0
    for op in STEPS[last]:
        yield op, c, t, k
        c += is_chain(op)
        t += is_turn(op)
        k += is_chain(op) and op[0] == "chain"


def piece_of(name):
    return {"k": 0, "v": 1}[name] if name in "kv" else 2 + int(name[1:])


def columns(piece):
    p = PROJ_ORDER[piece]
    return slice(p * P, (p + 1) * P)


def unit_of(u):
    return u // UNITS % BATCH, u // TOK_TILES % QPG, u % TOK_TILES


def products(pe, dst, pairs):
    for n, (lhs, rhs) in enumerate(pairs):
        last = pe.matmul(dst, lhs, rhs, start=(n == 0), stop=(n == len(pairs) - 1))
    return last


def turned(pe, dst, src, ident):
    return pe.matmul(dst, src, ident, start=True, stop=True, is_transpose=True)


def normalise(eng, count, src, st, first, n, s_var, s_pow, pow_value):
    tiles = slice(first, first + n)
    ve, rstd, nt = st["ve"][:, tiles], st["rstd"][:, tiles], st["nt"][:, tiles]
    for t in range(n):
        ready = count.mark(eng.bn_stats(st["stats"][:, first + t, :], src[:, t, :]))
    eng.wait_ge(count.sem, ready)
    count.mark(eng.memset(nt, 0.0))
    for t in range(first, first + n):
        ready = count.mark(eng.bn_aggr(st["mv"][:, t, :], st["stats"][:, t, :]))
    eng.wait_ge(count.sem, ready)
    eng.tensor_scalar(ve, st["mv"][:, tiles, 1], EPS, None, ALU.add).then_inc(s_var, 1)
    eng.wait_ge(s_pow, pow_value)
    count.seal(eng, eng.tensor_tensor(nt, rstd, rstd, ALU.mult))
    count.seal(eng, eng.tensor_tensor(nt, nt, ve, ALU.mult))
    count.seal(eng, eng.tensor_scalar(nt, nt, -0.5, 1.5, ALU.mult, ALU.add))
    count.seal(eng, eng.tensor_tensor(rstd, rstd, nt, ALU.mult))


NORM_MARKS = 2 * TOK_TILES + 5

RESULT_MARKS = 1 + TOK_TILES

KV, XG, XD = 8, 4, 16
X_SCALE = XD ** -0.5
SLOT = 64
X_ONE = 3 * XD
X_MARKS = KV * RESULT_MARKS + NORM_MARKS
ITEMS = BATCH * KV
VW = 32


def cross_steps(kv, m_left):
    turns = {0: ("k", 0, 2), 1: ("q", 0, 2), 2: ("m", 1, 0), 3: ("k", 1, 2), 4: ("q", 1, 2), 5: ("o", 0, -2),
             7: ("m", 0, 1)}
    ops = []
    s_units = iter(range(XG * TOK_TILES))
    for k in range(8):
        if m_left >= 0:
            ops.append(("st", k))
        if m_left >= 1:
            ops += [("s", next(s_units)) for _ in range({0: 3, 1: 3, 7: 0}.get(k, 2))]
        if k in turns and (m_left >= turns[k][2] if turns[k][0] != "o" else kv >= 2):
            ops.append(("t",) + turns[k])
        if kv >= 1 and m_left >= -1 and k % 2:
            ops.append(("pv", k // 2))
    return ops


TA_START, TA_ITEM = 9, 6


EXPERTS, WIDE, SHARED = 8, 352, 704
ROWS = EXPERTS * WIDE + SHARED
PAIR = 2 * P
N_PAIR = 2 * (-(-ROWS // (2 * PAIR)))
ROWS_PAD = N_PAIR * PAIR
KINDS = EXPERTS + 1
PARTS = 3 * KINDS


def ffn_steps(first, last):
    ops = []
    for half in range(2):
        for ch in range(BATCH):
            q = half * BATCH + ch
            more = not (last and q == 2 * BATCH - 1)
            for i in range(2):
                if more:
                    ops.append(("h", q + 1, i))
                ops += [("y", q, 2 * i), ("y", q, 2 * i + 1)]
            if ch < 3 and not (last and half == 1):
                ops.append(("w", half, ch))
    return ops


def over_pairs(eng, body):
    with eng.Fori(0, N_PAIR // 2 - 1) as g:
        body(g, False)
    body(N_PAIR // 2 - 1, True)


def over_items(item):
    def batch(b, before, left):
        for kv in range(KV):
            item(b, kv, cross_steps(before + kv, left - kv))

    def run(eng):
        batch(0, 0, ITEMS)
        with eng.Fori(1, BATCH - 1) as b:
            batch(b, KV, ITEMS)
        batch(BATCH - 1, KV, KV - 1)
        for kv in range(2):
            item(BATCH, kv, cross_steps(KV, -1 - kv))
    return run


def build(nc, x, ctx_in, w_qkv_t, w_proj_t, gate_t, w1_t, w2_t, w3_t, kinds, out, phases="ABC"):
    x_v = x.rearrange("b (t p) c -> b p t c", p=P)
    ctx_v = ctx_in.rearrange("b (t p) c -> b p t c", p=P)
    w1_v = w1_t.rearrange("(c p) (g n) -> g p c n", p=P, g=N_PAIR)
    w2_v = w2_t.rearrange("(c p) (g n) -> g p c n", p=P, g=N_PAIR)
    w3_v = w3_t.rearrange("(g i p) n -> g p i n", p=P, g=N_PAIR)
    kinds_v = kinds.rearrange("k (g n) -> g k n", g=N_PAIR)
    gate_v = gate_t.rearrange("(c p) e -> p c e", p=P)
    out_v = out.rearrange("b (t p) c -> b p t c", p=P)
    w_v = w_qkv_t.rearrange("(c p) (g n) -> g p c n", p=P, g=GROUPS)
    wo_v = w_proj_t.rearrange("(g h p) n -> g p h n", p=P, g=GROUPS)

    with ExitStack() as whole:
        def sem(name):
            return whole.enter_context(nc.semaphore(name))

        def keep(name, shape, dt=F32):
            return whole.enter_context(nc.sbuf_tensor(name, shape, dt))

        ps = whole.enter_context(nc.psum_tensor("ps", [P, 8, 512], F32))
        res = keep("res", [P, TILES, HID])
        ident = keep("ident", [P, P])
        norm = {n: keep(n, [P, TILES] + w) for n, w in (("stats", [6]), ("mv", [2]), ("ve", []), ("rstd", []),
                                                        ("nt", []))}
        mv, rstd = norm["mv"], norm["rstd"]
        ones = keep("ones", [P, 1])
        half = keep("half", [P, TOK_TILES])

        s_x = [sem(f"s_x{b}") for b in range(BATCH)]
        s_cst = sem("s_cst")
        s_dve = sem("s_dve")
        s_var = sem("s_var")
        s_pow = sem("s_pow")
        s_xn = sem("s_xn")
        s_xt = sem("s_xt")
        s_xh = sem("s_xh")
        s_xl = sem("s_xl")
        s_out = sem("s_out")

        s_w = sem("s_w")
        s_wh = sem("s_wh")
        s_wl = sem("s_wl")
        s_s = sem("s_s")
        s_max = sem("s_max")
        s_exp = sem("s_exp")
        s_pn = sem("s_pn")
        s_t = sem("s_t")
        s_te = sem("s_te")
        s_pv = sem("s_pv")
        s_ah = sem("s_ah")
        s_al = sem("s_al")
        s_g = sem("s_g")
        s_q = sem("s_q")
        s_res = sem("s_res")
        S_BANK, T_BANK, O_BANK, G_BANK = 0, 2, 4, 6

        s_ctx = sem("s_ctx")
        s_pc = sem("s_pc")
        s_px = sem("s_px")
        s_pm = sem("s_pm")
        s_kc = sem("s_kc")
        s_xq = sem("s_xq")
        s_vx = sem("s_vx")
        s_xn2 = sem("s_xn2")
        s_xmax = sem("s_xmax")
        s_mq = sem("s_mq")
        s_kt = sem("s_kt")
        s_qt = sem("s_qt")
        s_mt = sem("s_mt")
        s_ot = sem("s_ot")
        s_ta = sem("s_ta")
        s_to = sem("s_to")
        s_xs = sem("s_xs")
        s_st = sem("s_st")
        s_xe = sem("s_xe")
        s_xpv = sem("s_xpv")
        s_oe = sem("s_oe")
        s_gw = sem("s_gw")
        s_gs = sem("s_gs")
        s_fn = sem("s_fn")
        s_ft = sem("s_ft")
        s_fh = sem("s_fh")
        s_fl = sem("s_fl")
        s_lg = sem("s_lg")
        s_la = sem("s_la")
        s_lb = sem("s_lb")
        s_cp = sem("s_cp")
        s_ct = sem("s_ct")
        s_ce = sem("s_ce")
        s_fw = sem("s_fw")
        s_wa = sem("s_wa")
        s_wb = sem("s_wb")
        s_h1 = sem("s_h1")
        s_h2 = sem("s_h2")
        s_si = sem("s_si")
        s_pr = sem("s_pr")
        s_hd = sem("s_hd")
        s_hh = sem("s_hh")
        s_hl = sem("s_hl")
        s_y = sem("s_y")
        s_yr = sem("s_yr")
        H1, H2, HC, HY = 0, 2, 4, 6
        XST, XS, XO, XT = 0, 4, 6, 7

        pa = ExitStack()

        def sba(name, shape, dt=F32):
            return pa.enter_context(nc.sbuf_tensor(name, shape, dt))

        xh = sba("xh", [P, KC, BATCH * SEQ], F32R)
        xl = sba("xl", [P, KC, BATCH * SEQ], F32R)
        w_raw = sba("w_raw", [P, KC, NPROJ * P])
        wo_raw = w_raw[:, :, :].rearrange("p c n -> p (c n)")[:, 0:QPG * HID].rearrange("p (h n) -> p h n", h=QPG)
        wh = sba("wh", [P, KC, NPROJ * P], F32R)
        wl = sba("wl", [P, KC, NPROJ * P], F32R)
        woh = sba("woh", [P, QPG, HID], F32R)
        wol = sba("wol", [P, QPG, HID], F32R)
        q_t = sba("q_t", [P, 2, QPG, SEQ])
        k_t = sba("k_t", [P, 2, SEQ])
        v_t = sba("v_t", [P, SEQ])
        v_s = sba("v_s", [P, 2, TOK_TILES, D])
        probs = sba("probs", [P, 4, SEQ])
        pt = sba("pt", [P, TOK_TILES, SEQ])
        ah = sba("ah", [P, QPG, SEQ], F32R)
        al = sba("al", [P, QPG, SEQ], F32R)
        mask = sba("mask", [P, P], BF16)
        ident_b = sba("ident_b", [P, P], BF16)
        nmax = sba("nmax", [P, 4])
        rsum = sba("rsum", [P, 4])
        rinv = sba("rinv", [P, 4])
        pa.close()

        pb = ExitStack()

        def sbb(name, shape, dt=F32):
            return pb.enter_context(nc.sbuf_tensor(name, shape, dt))

        xn = sbb("xn", [P, TOK_TILES, HID])
        kc = sbb("kc", [P, TOK_TILES, KV, 3 * SLOT])
        ctx_s = sbb("ctx_s", [P, TOK_TILES, KV * XD])
        xq = sbb("xq", [P, 4, TOK_TILES, XG, SLOT])
        vx = sbb("vx", [P, 4, TOK_TILES, VW])
        k3 = sbb("k3", [P, 4, 2, SEQ], F32R)
        q3 = sbb("q3", [P, 2, 2, SEQ], F32R)
        q3m = sbb("q3m", [P, 2, SEQ], F32R)
        o_t = sbb("o_t", [P, 2, SEQ])
        xmax = sbb("xmax", [P, 2, TOK_TILES, XG])
        xrec = sbb("xrec", [P, TOK_TILES, XG])
        xo = sbb("xo", [P, TOK_TILES, XG, XD])
        xp = sbb("xp", [P, 2, XG, TOK_TILES, SEQ])
        pb.close()

        pc = ExitStack()

        def sbc(name, shape, dt=F32):
            return pc.enter_context(nc.sbuf_tensor(name, shape, dt))

        fh = sbc("fh", [P, KC, BATCH * SEQ], F32R)
        fl = sbc("fl", [P, KC, BATCH * SEQ], F32R)
        fn = sbc("fn", [P, 2, HID])
        w12_raw = sbc("w12_raw", [P, KC, 2, PAIR])
        w3_raw = sbc("w3_raw", [P, 2, HID])
        kind_raw = sbc("kind_raw", [PARTS, PAIR], BF16)
        w12h = sbc("w12h", [P, 2, KC, 2, PAIR], F32R)
        w12l = sbc("w12l", [P, 2, KC, 2, PAIR], F32R)
        w3h = sbc("w3h", [P, 2, 2, HID], F32R)
        w3l = sbc("w3l", [P, 2, 2, HID], F32R)
        kind_s = sbc("kind_s", [PARTS, 2, PAIR], BF16)
        comb_t = sbc("comb_t", [PARTS, BATCH * SEQ], BF16)
        act_s = sbc("act_s", [P, 2, SEQ])
        prod = sbc("prod", [P, 2, SEQ])
        hid = sbc("hid", [P, 2, SEQ])
        hh = sbc("hh", [P, 2, 2, SEQ], F32R)
        hl = sbc("hl", [P, 2, 2, SEQ], F32R)
        gate_raw = sbc("gate_raw", [P, KC, EXPERTS])
        gate_s = sbc("gate_s", [P, KC, 2 * EXPERTS], F32R)
        glow = sbc("glow", [P, TILES, EXPERTS])
        logit = sbc("logit", [P, TILES, EXPERTS])
        gprob = sbc("gprob", [P, TILES, EXPERTS])
        gmax = sbc("gmax", [P, TILES])
        top = sbc("top", [P, TILES, 8])
        top_i = sbc("top_i", [P, TILES, 8], mybir.dt.uint32)
        top_f = sbc("top_f", [P, TILES, 8])
        number = sbc("number", [P, EXPERTS])
        pick = sbc("pick", [P, 2, TILES, EXPERTS])
        comb = sbc("comb", [P, TILES, KINDS])
        comb_h = sbc("comb_h", [P, TILES, KINDS], BF16)
        comb_m = sbc("comb_m", [P, TILES, KINDS], BF16)
        parts = sbc("parts", [P, TILES, PARTS])
        pc.close()

        gate_ps = ps[:, H2, 0:2 * EXPERTS * TILES].rearrange("p (t e) -> p t e", t=TILES)
        block = whole.enter_context(nc.Block())

        @block.sync
        def _(sp):
            for b in range(BATCH):
                sp.dma_start(res[:, b * TOK_TILES:(b + 1) * TOK_TILES, :], x_v[b]).then_inc(s_x[b], 16)
                if b == 0:
                    sp.dma_start(w_raw[:, :, :], w_v[0]).then_inc(s_w, 16)
            sp.wait_ge(s_wl, NPROJ)
            sp.dma_start(wo_raw, wo_v[0]).then_inc(s_w, 16)
            with sp.Fori(0, GROUPS - 1) as g:
                sp.wait_ge(s_wl, N_SPLIT * g + N_SPLIT)
                sp.dma_start(w_raw[:, :, :], w_v[g + 1]).then_inc(s_w, 16)
                sp.wait_ge(s_wl, N_SPLIT * g + N_SPLIT + NPROJ)
                sp.dma_start(wo_raw, wo_v[g + 1]).then_inc(s_w, 16)
            if phases != "A":
                sp.wait_ge(s_q, N_QKV * GROUPS)
                sp.dma_start(ctx_s[:, :, :], ctx_v[0]).then_inc(s_ctx, 16)
                with sp.Fori(0, BATCH - 1) as b:
                    sp.wait_ge(s_kc, TOK_TILES * b + TOK_TILES)
                    sp.dma_start(ctx_s[:, :, :], ctx_v[b + 1]).then_inc(s_ctx, 16)
            if phases == "ABC":
                def load_pair(g):
                    sp.dma_start(w12_raw[:, :, 0, :], w1_v[g]).then_inc(s_fw, 16)
                    sp.dma_start(w12_raw[:, :, 1, :], w2_v[g]).then_inc(s_fw, 16)
                    sp.dma_start(w3_raw[:, :, :], w3_v[g]).then_inc(s_fw, 16)
                    sp.dma_start(kind_raw[:, :], kinds_v[g]).then_inc(s_fw, 16)

                sp.wait_ge(s_to, ITEMS)
                sp.dma_start(gate_raw[:, :, :], gate_v).then_inc(s_gw, 16)
                load_pair(0)
                with sp.Fori(0, N_PAIR - 1) as g:
                    sp.wait_ge(s_wb, 3 * g + 3)
                    load_pair(g + 1)
                for b in range(BATCH):
                    sp.wait_ge(s_yr, 2 + TILES * (N_PAIR - 1) + (b + 1) * TOK_TILES)
                    sp.dma_start(out_v[b], res[:, b * TOK_TILES:(b + 1) * TOK_TILES, :]).then_inc(s_out, 16)
                sp.wait_ge(s_out, 16 * BATCH)
            if phases == "AB":
                for b in range(BATCH):
                    sp.wait_ge(s_to, KV * (b + 1))
                    sp.dma_start(out_v[b], res[:, b * TOK_TILES:(b + 1) * TOK_TILES, :]).then_inc(s_out, 16)
                sp.wait_ge(s_out, 16 * BATCH)
            if phases == "A":
                for b in range(BATCH):
                    sp.wait_ge(s_res, (GROUPS - 1) * TILES + (b + 1) * TOK_TILES + 1)
                    sp.dma_start(out_v[b], res[:, b * TOK_TILES:(b + 1) * TOK_TILES, :]).then_inc(s_out, 16)
                sp.wait_ge(s_out, 16 * BATCH)

        @block.gpsimd
        def _(pool):
            pool.memset(ident[:, :], 0.0).then_inc(s_cst, 1)
            pool.memset(ident_b[:, :], 0.0).then_inc(s_cst, 1)
            pool.memset(mask[:, :], 0.0).then_inc(s_cst, 1)
            pool.memset(half[:, :], -0.5).then_inc(s_cst, 1)
            pool.memset(ones[:, :], 1.0).then_inc(s_cst, 1)
            pool.wait_ge(s_cst, 5)
            for t in (ident, ident_b):
                pool.affine_select(out=t[:, :], in_=t[:, :], compare_op=ALU.not_equal, fill=1.0, base=0,
                                   pattern=[[-1, P]], channel_multiplier=1).then_inc(s_cst, 1)
            pool.affine_select(out=mask[:, :], in_=mask[:, :], compare_op=ALU.is_ge, fill=MASKED, base=0,
                               pattern=[[-1, P]], channel_multiplier=1).then_inc(s_cst, 1)

            def power(b, value):
                tiles = slice(b * TOK_TILES, (b + 1) * TOK_TILES)
                pool.wait_ge(s_var, value)
                pool.tensor_tensor(rstd[:, tiles], norm["ve"][:, tiles], half[:, :], ALU.pow).then_inc(s_pow, 1)

            for b in range(BATCH):
                power(b, b + 1)
            if phases == "A":
                return

            pool.wait_ge(s_q, N_QKV * GROUPS)
            pool.memset(kc[:, :, :, :], 0.0).then_inc(s_pc, 1)
            pool.memset(xq[:, :, :, :, :], 0.0).then_inc(s_pc, 1)
            pool.memset(vx[:, :, :, :], 0.0).then_inc(s_pc, 1)
            pool.wait_ge(s_pc, 3)
            pool.memset(kc[:, :, :, SLOT + X_ONE:SLOT + X_ONE + 2], 1.0).then_inc(s_pc, 1)
            pool.memset(vx[:, :, :, XD:XD + 1], 1.0).then_inc(s_pc, 1)
            pool.wait_ge(s_pc, 5)
            ctx_h = ctx_s[:, :, :].rearrange("p t (k d) -> p t k d", k=KV)

            def high(dst, src, shape):
                one = ones[:, :].unsqueeze(2).to_broadcast([P] + list(shape))
                return pool.tensor_tensor(dst.bitcast(F32R), src, one, ALU.mult)

            def build_keys(b):
                pool.wait_ge(s_ctx, 16 * b + 16)
                at = kc[:, :, :, SLOT:2 * SLOT]
                for i in range(TOK_TILES):
                    for n in (0, 2):
                        high(at[:, i, :, n * XD:(n + 1) * XD], ctx_h[:, i], (KV, XD)).then_inc(s_pc, 1)
                pool.wait_ge(s_pc, 5 + 8 * b + 8)
                for i in range(TOK_TILES):
                    pool.tensor_tensor(at[:, i, :, XD:2 * XD].bitcast(F32R), ctx_h[:, i], at[:, i, :, 0:XD],
                                       ALU.subtract).then_inc(s_kc, 1)

            def build_queries(slot, kv, value):
                src = xn[:, :, kv * XG * XD:(kv + 1) * XG * XD].rearrange("p t (h d) -> p t h d", h=XG)
                for n in (0, 1):
                    for i in range(TOK_TILES):
                        high(xq[:, slot, i, :, n * XD:(n + 1) * XD], src[:, i], (XG, XD)).then_inc(s_px, 1)
                pool.memset(xq[:, slot, :, :, X_ONE:X_ONE + 2], 0.0).then_inc(s_px, 1)
                pool.wait_ge(s_px, value)
                for i in range(TOK_TILES):
                    pool.tensor_tensor(xq[:, slot, i, :, 2 * XD:3 * XD].bitcast(F32R), src[:, i],
                                       xq[:, slot, i, :, 0:XD], ALU.subtract).then_inc(s_xq, 1)

            def build_values(kv):
                pool.tensor_tensor(vx[:, kv % 4, :, 0:XD], kc[:, :, kv, SLOT:SLOT + XD],
                                   kc[:, :, kv, SLOT + XD:SLOT + 2 * XD], ALU.add).then_inc(s_vx, 1)

            def put_maxima(slot, pair, units, value):
                pool.wait_ge(s_xmax, units)
                heads = slice(2 * pair, 2 * pair + 2)
                high(xq[:, slot, :, heads, X_ONE], xmax[:, slot % 2, :, heads], (TOK_TILES, 2)).then_inc(s_pm, 1)
                pool.wait_ge(s_pm, value)
                pool.tensor_tensor(xq[:, slot, :, heads, X_ONE + 1].bitcast(F32R), xmax[:, slot % 2, :, heads],
                                   xq[:, slot, :, heads, X_ONE], ALU.subtract).then_inc(s_mq, 1)

            build_keys(0)
            pool.wait_ge(s_kc, TOK_TILES)
            build_values(0)
            build_values(1)
            power(0, BATCH + 1)
            pool.wait_ge(s_xn2, TOK_TILES)
            for kv in range(3):
                build_queries(kv, kv, 9 * kv + 9)
            put_maxima(0, 0, 2 * TOK_TILES, 1)
            put_maxima(0, 1, 4 * TOK_TILES, 2)

            def cross(b, first, last):
                for kv in range(KV):
                    m = KV * b + kv
                    if not (last and kv >= KV - 3):
                        if kv == KV - 3:
                            pool.wait_ge(s_xn2, TOK_TILES * b + 2 * TOK_TILES)
                        if not (first and kv == 0):
                            pool.wait_ge(s_mt, 2 * m)
                        build_queries((kv + 3) % 4, (kv + 3) % KV, 9 * m + 36)
                    if kv == 1 and not last:
                        power_next(b)
                    if not (last and kv >= KV - 2):
                        if kv == KV - 2:
                            pool.wait_ge(s_kc, TOK_TILES * b + 2 * TOK_TILES)
                        if not (first and kv < 2):
                            pool.wait_ge(s_xpv, m - 1)
                        build_values((kv + 2) % KV)
                    if kv == KV - 3 and not last:
                        pool.wait_ge(s_kt, 2 * m + 6)
                        pool.wait_ge(s_vx, m + 3)
                        build_keys(b + 1)
                    if not (last and kv == KV - 1):
                        put_maxima((kv + 1) % 4, 0, 16 * m + 24, 2 * m + 3)
                        put_maxima((kv + 1) % 4, 1, 16 * m + 32, 2 * m + 4)

            def power_next(b):
                tiles = slice(0, TOK_TILES)
                pool.wait_ge(s_var, BATCH + b + 2)
                pool.tensor_tensor(rstd[:, tiles], norm["ve"][:, tiles], half[:, :], ALU.pow).then_inc(s_pow, 1)

            cross(0, True, False)
            with pool.Fori(1, BATCH - 1) as b:
                cross(b, False, False)
            cross(BATCH - 1, False, True)
            if phases == "AB":
                return

            pool.wait_ge(s_to, ITEMS)
            for e in range(EXPERTS):
                pool.memset(number[:, e:e + 1], float(e)).then_inc(s_cst, 1)
            pool.memset(comb[:, :, EXPERTS:KINDS], 1.0).then_inc(s_cst, 1)
            for b in range(BATCH):
                power(b, 2 * BATCH + b + 1)

            def low(n, slot, i):
                pool.wait_ge(s_hh, n + 1)
                pool.tensor_tensor(hl[:, slot, i, :], hid[:, i, :], hh[:, slot, i, :].bitcast(F32), ALU.subtract)\
                    .then_inc(s_hl, 1)

            low(0, 0, 0)
            low(1, 0, 1)

            def pairs(g, last):
                for op in ffn_steps(False, last):
                    if op[0] == "h":
                        low(4 * BATCH * g + 2 * op[1] + op[2], op[1] % 2, op[2])

            over_pairs(pool, pairs)

        @block.tensor
        def _(pe):
            pe.wait_ge(s_cst, 8)
            for t in range(TILES):
                pe.wait_ge(s_xn, t + 1)
                if t >= 2:
                    pe.wait_ge(s_xl, t - 1)
                for c in range(KC):
                    last = turned(pe, ps[:, S_BANK + t % 2, c * P:(c + 1) * P],
                                        probs[:, t % 2, c * P:(c + 1) * P], ident[:, :])
                last.then_inc(s_xt, 1)

            def project(piece, b, bank):
                toks = slice(b * SEQ, (b + 1) * SEQ)
                products(pe, ps[:, G_BANK + bank, :],
                         [(w[:, c, columns(piece)], xx[:, c, toks])
                          for w, xx in ((wh, xh), (wl, xh), (wh, xl)) for c in range(KC)]).then_inc(s_g, 1)

            def turn_v(bank):
                for t in range(TOK_TILES):
                    last = turned(pe, ps[:, T_BANK + bank, t * P:(t + 1) * P], v_t[:, t * P:(t + 1) * P], ident[:, :])
                last.then_inc(s_t, 1)

            def scores(u):
                b, h, i = unit_of(u)
                w = (i + 1) * P
                pe.matmul(ps[:, S_BANK + u % 2, i * P:w], ident_b[:, :], mask[:, :], start=True, stop=True)
                pe.matmul(ps[:, S_BANK + u % 2, 0:w], q_t[:, b % 2, h, i * P:w], k_t[:, b % 2, 0:w],
                          start=False, stop=True, skip_group_check=True).then_inc(s_s, 1)

            pe.wait_ge(s_xl, TILES)
            for n in range(NPROJ):
                pe.wait_ge(s_wl, n + 1)
                if n >= 2:
                    pe.wait_ge(s_q, n - 1)
                project(n, 0, n % 2)
            pe.wait_ge(s_q, 2)
            turn_v(0)
            pe.wait_ge(s_q, 3)
            scores(0)

            def chain_taken(g, last, c):
                if c < 2:
                    pe.wait_ge(s_q, N_QKV * g + NPROJ)
                    pe.wait_ge(s_res, TILES * g + 1)
                    return
                before = [(op, k) for op, n, t, k in walk(last) if is_chain(op) and n == c - 2][0]
                if before[0][0] == "out":
                    pe.wait_ge(s_res, TILES * g + before[0][2] * TOK_TILES + before[0][1] + 2)
                else:
                    pe.wait_ge(s_q, N_QKV * g + NPROJ + before[1] + 1)

            def group(g, last):
                for op, c, t, k in walk(last):
                    if op[0] == "score":
                        u = op[1]
                        if u % TOK_TILES == 0:
                            pe.wait_ge(s_q, N_QKV * g + NPROJ * (u // UNITS) + 3 + unit_of(u)[1])
                        pe.wait_ge(s_exp, N_UNIT * g + u)
                        scores(u)
                    elif op[0] == "turn":
                        pe.wait_ge(s_pn, N_UNIT * g + op[1] + 1)
                        pe.wait_ge(s_te, N_TURN * g + t + 1)
                        for j in range(op[1] % TOK_TILES + 1):
                            ins = turned(pe, ps[:, T_BANK + (1 + t) % 2, j * P:(j + 1) * P],
                                               probs[:, op[1] % 4, j * P:(j + 1) * P], ident[:, :])
                        ins.then_inc(s_t, 1)
                    elif op[0] == "pv":
                        b, h = op[1] // QPG, op[1] % QPG
                        pe.wait_ge(s_te, N_TURN * g + t + 2)
                        for j in reversed(range(TOK_TILES)):
                            ins = pe.matmul(ps[:, O_BANK + h % 2, j * P:], v_s[:, b % 2, j, :], pt[:, j, j * P:],
                                            start=(j == TOK_TILES - 1), stop=True, skip_group_check=True)
                        ins.then_inc(s_pv, 1)
                    elif op[0] == "out":
                        i, b = op[1:]
                        if i == 0:
                            pe.wait_ge(s_al, N_HEAD * g + QPG * (b + 1))
                            pe.wait_ge(s_wl, N_SPLIT * g + N_SPLIT)
                        chain_taken(g, last, c)
                        toks = slice(i * P, (i + 1) * P)
                        products(pe, ps[:, G_BANK + c % 2, :],
                                 [(a[:, h, toks], w[:, h, :])
                                  for a, w in ((ah, woh), (ah, wol), (al, woh)) for h in range(QPG)]).then_inc(s_g, 1)
                    elif is_chain(op):
                        n = piece_of(op[1])
                        if op[2] == 0:
                            pe.wait_ge(s_wl, N_SPLIT * g + N_SPLIT + n + 1)
                        chain_taken(g, last, c)
                        project(n, op[2], c % 2)
                    elif op[0] == "chain":
                        pe.wait_ge(s_q, NPROJ + N_QKV * g + k - 1)
                        pe.wait_ge(s_te, N_TURN * g + t + 1)
                        turn_v((1 + t) % 2)

            with pe.Fori(0, GROUPS - 1) as g:
                group(g, False)
            group(GROUPS - 1, True)
            if phases == "A":
                return

            pe.wait_ge(s_res, GROUPS * TILES + 1)

            def cross(b, kv, steps):
                m = KV * b + kv
                now, ahead2 = ("st", 0) in steps, ("t", "k", 0, 2) in steps
                taken = TA_START + TA_ITEM * m
                if isinstance(m, int) and m == ITEMS - 1:
                    taken -= 4
                start = taken
                before_is_result = not now
                for op in steps:
                    if op[0] == "t":
                        kind, which, off = op[1:]
                        if before_is_result:
                            pe.wait_ge(s_to, m - 1 if kind != "o" else m - 2)
                        else:
                            pe.wait_ge(s_ta, taken)
                        before_is_result = kind == "o"
                        taken = taken + (kind != "o")
                        slot = (kv + off) % 4
                        if kind == "k":
                            pe.wait_ge(s_kc, TOK_TILES * (b + (kv + 2) // KV) + TOK_TILES)
                            for i in range(TOK_TILES):
                                src = kc[:, i, (kv + off) % KV, SLOT * (1 - which):SLOT * (3 - which)]
                                ins = turned(pe, ps[:, XT, i * P:(i + 1) * P], src, ident[:, :])
                            ins.then_inc(s_kt, 1)
                        elif kind in "qm":
                            if kind == "q":
                                pe.wait_ge(s_xq, TOK_TILES * m + 3 * TOK_TILES)
                            else:
                                pe.wait_ge(s_mq, 2 * (m + off) + which + 1)
                            for i in range(TOK_TILES):
                                src = xq[:, slot, i, 2 * which:2 * which + 2, :].rearrange("p h c -> p (h c)")
                                ins = turned(pe, ps[:, XT, i * P:(i + 1) * P], src, ident[:, :])
                            ins.then_inc(s_qt if kind == "q" else s_mt, 1)
                        else:
                            pe.wait_ge(s_oe, m - 1)
                            for i in range(TOK_TILES):
                                ins = turned(pe, ps[:, XT, i * P:(i + 1) * P], o_t[:, kv % 2, i * P:(i + 1) * P],
                                             ident[:, :])
                            ins.then_inc(s_ot, 1)
                    elif op[0] == "s":
                        h, i = op[1] // TOK_TILES, op[1] % TOK_TILES
                        if op[1] == 0:
                            pe.wait_ge(s_ta, start - 1)
                        pe.wait_ge(s_xmax, 16 * m + 16 + op[1] - 1)
                        pe.matmul(ps[:, XS + op[1] % 2, :], q3[:, (kv + 1) % 2, h // 2, i * P:(i + 1) * P],
                                  k3[:, (kv + 1) % 4, h % 2, :], start=True, stop=True).then_inc(s_xs, 1)
                    elif op[0] == "st":
                        h, pair = op[1] // 2, op[1] % 2
                        if op[1] == 0:
                            pe.wait_ge(s_ta, taken)
                        if op[1] == 4:
                            pe.wait_ge(s_ta, start + (3 if ahead2 else 1))
                        if not (isinstance(m, int) and 8 * m + op[1] < 2):
                            pe.wait_ge(s_xe, 8 * m + op[1] - 1)
                        for e in range(2):
                            t = 2 * pair + e
                            ins = pe.matmul(ps[:, XST + 2 * pair + e, :], k3[:, kv % 4, h % 2, t * P:(t + 1) * P],
                                            q3m[:, h // 2, :], start=True, stop=True)
                        ins.then_inc(s_st, 1)
                    else:
                        j, before = op[1], (kv - 1) % KV
                        if j == 0:
                            pe.wait_ge(s_vx, m)
                            if not (isinstance(m, int) and m < 2):
                                pe.wait_ge(s_oe, m - 1)
                        pe.wait_ge(s_xe, 8 * m - (1 if j < 2 else 0))
                        for h in range(XG):
                            ins = pe.matmul(ps[VW * h:VW * (h + 1), XO, :], vx[:, before % 4, j, :],
                                            xp[:, (kv - 1) % 2, h, j, :], start=(j == 0), stop=(j == TOK_TILES - 1),
                                            tile_position=(0, VW * h))
                        if j == TOK_TILES - 1:
                            ins.then_inc(s_xpv, 1)

            def turn_first(kind, which, item, wait, ready, done, n):
                pe.wait_ge(wait, ready)
                if n:
                    pe.wait_ge(s_ta, n)
                for i in range(TOK_TILES):
                    src = kc[:, i, item, SLOT * (1 - which):SLOT * (3 - which)] if kind == "k" else \
                        xq[:, item, i, 2 * which:2 * which + 2, :].rearrange("p h c -> p (h c)")
                    ins = turned(pe, ps[:, XT, i * P:(i + 1) * P], src, ident[:, :])
                ins.then_inc(done, 1)

            for item in range(2):
                for which in range(2):
                    turn_first("k", which, item, s_kc, TOK_TILES, s_kt, 4 * item + 2 * which)
                    turn_first("q", which, item, s_xq, TOK_TILES * (item + 1), s_qt, 4 * item + 2 * which + 1)
                if item == 0:
                    pe.wait_ge(s_ta, 4)
                    for u in range(XG * TOK_TILES):
                        if u >= 2:
                            pe.wait_ge(s_xmax, u - 1)
                        h, i = u // TOK_TILES, u % TOK_TILES
                        pe.matmul(ps[:, XS + u % 2, :], q3[:, 0, h // 2, i * P:(i + 1) * P], k3[:, 0, h % 2, :],
                                  start=True, stop=True).then_inc(s_xs, 1)
            turn_first("m", 0, 0, s_mq, 1, s_mt, 8)

            over_items(cross)(pe)
            if phases == "AB":
                return

            pe.wait_ge(s_to, ITEMS)
            for t in range(TILES):
                pe.wait_ge(s_fn, t + 1)
                if t >= 2:
                    pe.wait_ge(s_fl, t - 1)
                for c in range(KC):
                    ins = turned(pe, ps[:, H1 + t % 2, c * P:(c + 1) * P], fn[:, t % 2, c * P:(c + 1) * P], ident[:, :])
                ins.then_inc(s_ft, 1)
            pe.wait_ge(s_gs, 2)
            for t in range(TILES):
                pe.wait_ge(s_fl, t + 1)
                toks = slice(t * P, (t + 1) * P)
                at = ps[:, H2, 2 * EXPERTS * t:2 * EXPERTS * (t + 1)]
                for c in range(KC):
                    pe.matmul(at, fh[:, c, toks], gate_s[:, c, :], start=(c == 0), stop=True, skip_group_check=c > 0)
                for c in range(KC):
                    ins = pe.matmul(at[:, 0:EXPERTS], fl[:, c, toks], gate_s[:, c, 0:EXPERTS], start=False, stop=True,
                                    skip_group_check=True)
            ins.then_inc(s_lg, 1)

            def hidden(n, par, ch, i):
                rows = slice(i * P, (i + 1) * P)
                toks = slice(ch * SEQ, (ch + 1) * SEQ)
                for k, bank, free, ready in ((0, H1, s_si, s_h1), (1, H2, s_pr, None)):
                    if not (isinstance(n, int) and n < 2):
                        pe.wait_ge(free, n - 1)
                    last = products(pe, ps[:, bank + i, :],
                                    [(w[:, par, c, k, rows], f[:, c, toks])
                                     for w, f in ((w12h, fh), (w12l, fh), (w12h, fl)) for c in range(KC)])
                    if ready is not None:
                        last.then_inc(ready, 1)
                if not (isinstance(n, int) and n < 2):
                    pe.wait_ge(s_hd, n - 1)
                pe.matmul(ps[:, HC + i, :], kind_s[:, par, rows], comb_t[:, toks], start=True, stop=True)\
                    .then_inc(s_h2, 1)

            pe.wait_ge(s_wb, 3)
            pe.wait_ge(s_cp, 1)
            for b in range(BATCH):
                for t in range(b * TOK_TILES, (b + 1) * TOK_TILES):
                    i = t % TOK_TILES
                    ins = turned(pe, ps[0:PARTS, HC + b, i * P:(i + 1) * P], parts[:, t, :], ident[:, :])
                ins.then_inc(s_ct, 1)
            pe.wait_ge(s_ce, BATCH)
            hidden(0, 0, 0, 0)
            hidden(1, 0, 0, 1)

            def pairs(g, last):
                for op in ffn_steps(False, last):
                    if op[0] == "h":
                        q, i = op[1:]
                        if q % BATCH == 0 and i == 0:
                            pe.wait_ge(s_wb, 6 * g + 3 * (q // BATCH) + 3)
                        hidden(4 * BATCH * g + 2 * q + i, q // BATCH % 2, q % BATCH, i)
                    elif op[0] == "y":
                        q, t = op[1:]
                        if t == 0:
                            pe.wait_ge(s_hl, 4 * BATCH * g + 2 * q + 2)
                        pe.wait_ge(s_yr, 8 * BATCH * g + 4 * q + t + 1)
                        toks = slice(t * P, (t + 1) * P)
                        products(pe, ps[:, HY + t % 2, :],
                                 [(a[:, q % 2, i, toks], w[:, q // BATCH, i, :])
                                  for i in range(2) for a, w in ((hh, w3h), (hh, w3l), (hl, w3h))]).then_inc(s_y, 1)

            over_pairs(pe, pairs)

        @block.scalar
        def _(act):
            act.nop().then_inc(s_exp, 1)
            act.nop().then_inc(s_te, 1)
            for t in range(TILES):
                act.wait_ge(s_xt, t + 1)
                act.copy(xh[:, :, t * P:(t + 1) * P],
                         ps[:, S_BANK + t % 2, :].rearrange("p (c n) -> p c n", c=KC)).then_inc(s_xh, 1)

            def split_in(n):
                act.copy(wh[:, :, columns(n)], w_raw[:, :, columns(n)]).then_inc(s_wh, 1)

            def take(piece, b, bank):
                name = PROJ_ORDER[piece]
                src = ps[:, G_BANK + bank, :]
                if piece == 0:
                    ins = act.copy(k_t[:, b % 2, :], src)
                elif piece == 1:
                    ins = act.copy(v_t[:, :], src)
                else:
                    ins = act.mul(q_t[:, b % 2, name, :], src, ATT_SCALE)
                return ins

            def exponentials(g, u):
                w = (u % TOK_TILES + 1) * P
                act.wait_ge(s_max, N_UNIT * g + u + 1)
                act.activation(probs[:, u % 4, 0:w], ps[:, S_BANK + u % 2, 0:w], ACT.Exp,
                               bias=nmax[:, u % 4:u % 4 + 1], accum_out=rsum[:, u % 4:u % 4 + 1]).then_inc(s_exp, 1)

            act.wait_ge(s_w, 16)
            for n in range(NPROJ):
                split_in(n)
            for n in range(NPROJ):
                act.wait_ge(s_g, n + 1)
                take(n, 0, n % 2).then_inc(s_q, 1)
            act.wait_ge(s_t, 1)
            act.copy(v_s[:, 0, :, :], ps[:, T_BANK, :].rearrange("p (j d) -> p j d", j=TOK_TILES)).then_inc(s_te, 1)
            exponentials(0, 0)

            def group(g, last):
                for op, c, t, k in walk(last):
                    if op[0] == "score":
                        exponentials(g, op[1])
                    elif op[0] == "split_out":
                        if op[1] == 0:
                            act.wait_ge(s_w, 32 * g + 32)
                            act.wait_ge(s_g, NPROJ + N_CHAIN * g)
                        act.copy(woh[:, op[1], :], wo_raw[:, op[1], :]).then_inc(s_wh, 1)
                    elif op[0] == "split_in":
                        if op[1] == 0:
                            act.wait_ge(s_w, 32 * g + 48)
                        split_in(op[1])
                    elif op[0] == "turn":
                        i = op[1] % TOK_TILES
                        act.wait_ge(s_t, N_TURN * g + t + 2)
                        act.copy(pt[:, 0:i + 1, i * P:(i + 1) * P],
                                 ps[:, T_BANK + (1 + t) % 2, 0:(i + 1) * P].rearrange("p (j n) -> p j n", n=P))\
                           .then_inc(s_te, 1)
                    elif op[0] == "pv":
                        act.wait_ge(s_pv, N_HEAD * g + op[1] + 1)
                        act.copy(ah[:, op[1] % QPG, :], ps[:, O_BANK + op[1] % 2, :]).then_inc(s_ah, 1)
                    elif op[0] == "chain" and is_chain(op):
                        act.wait_ge(s_g, NPROJ + N_CHAIN * g + c + 1)
                        take(piece_of(op[1]), op[2], c % 2).then_inc(s_q, 1)
                    elif op[0] == "chain":
                        act.wait_ge(s_t, N_TURN * g + t + 2)
                        act.copy(v_s[:, op[2] % 2, :, :],
                                 ps[:, T_BANK + (1 + t) % 2, :].rearrange("p (j d) -> p j d", j=TOK_TILES))\
                           .then_inc(s_te, 1)

            with act.Fori(0, GROUPS - 1) as g:
                group(g, False)
            group(GROUPS - 1, True)
            if phases == "A":
                return

            def take_turned(kind, which, slot, value):
                act.wait_ge({"k": s_kt, "q": s_qt, "m": s_mt}[kind], value)
                dst = {"k": k3[:, slot, which, :], "q": q3[:, slot % 2, which, :], "m": q3m[:, which, :]}[kind]
                act.copy(dst, ps[:, XT, :]).then_inc(s_ta, 1)

            for item in range(2):
                for which in range(2):
                    for kind in "kq":
                        take_turned(kind, which, item, 2 * item + which + 1)
            take_turned("m", 0, 0, 1)

            def cross(b, kv, steps):
                m = KV * b + kv
                for op in steps:
                    if op[0] == "st":
                        h, pair = op[1] // 2, op[1] % 2
                        act.wait_ge(s_st, 8 * m + op[1] + 1)
                        act.activation(xp[:, kv % 2, h, 2 * pair:2 * pair + 2, :],
                                       ps[:, XST + 2 * pair:XST + 2 * pair + 2, :], ACT.Exp,
                                       scale=X_SCALE).then_inc(s_xe, 1)
                    elif op[0] == "t" and op[1] != "o":
                        kind, which, off = op[1:]
                        take_turned(kind, which, (kv + off) % 4, 2 * (m + off) + which + 1)
                    elif op == ("pv", TOK_TILES - 1):
                        act.wait_ge(s_xpv, m)
                        act.copy(o_t[:, (kv - 1) % 2, :], ps[:, XO, :]).then_inc(s_oe, 1)

            over_items(cross)(act)
            if phases == "AB":
                return

            act.wait_ge(s_gw, 16)
            act.copy(gate_s[:, :, 0:EXPERTS], gate_raw[:, :, :]).then_inc(s_gs, 1)
            for t in range(TILES):
                act.wait_ge(s_ft, t + 1)
                act.copy(fh[:, :, t * P:(t + 1) * P], ps[:, H1 + t % 2, :].rearrange("p (c n) -> p c n", c=KC))\
                   .then_inc(s_fh, 1)

            def split(par, n, value):
                if n < 2:
                    act.copy(w12h[:, par, :, n, :], w12_raw[:, :, n, :]).then_inc(s_wa, 1)
                else:
                    act.copy(kind_s[:, par, :], kind_raw[:, :]).then_inc(s_wa, 1)
                    act.copy(w3h[:, par, :, :], w3_raw[:, :, :]).then_inc(s_wa, 1)

            act.wait_ge(s_fw, 64)
            for n in range(3):
                split(0, n, n + 1)
            act.wait_ge(s_lg, 1)
            act.copy(glow[:, :, :], gate_ps[:, :, EXPERTS:]).then_inc(s_la, 1)
            act.wait_ge(s_lb, 1)
            act.activation(gprob[:, :, :], logit[:, :, :], ACT.Exp).then_inc(s_la, 1)
            for b in range(BATCH):
                act.wait_ge(s_ct, b + 1)
                act.copy(comb_t[:, b * SEQ:(b + 1) * SEQ], ps[0:PARTS, HC + b, :]).then_inc(s_ce, 1)

            def silu(n, i):
                act.wait_ge(s_h1, n + 1)
                act.activation(act_s[:, i, :], ps[:, H1 + i, :], ACT.Silu).then_inc(s_si, 1)

            def high(n, slot, i):
                act.wait_ge(s_hd, n + 1)
                act.copy(hh[:, slot, i, :], hid[:, i, :]).then_inc(s_hh, 1)

            for i in range(2):
                silu(i, i)
                high(i, 0, i)

            def pairs(g, last):
                for op in ffn_steps(False, last):
                    if op[0] == "h":
                        n = 4 * BATCH * g + 2 * op[1] + op[2]
                        silu(n, op[2])
                        high(n, op[1] % 2, op[2])
                    elif op[0] == "w":
                        if op[2] == 0:
                            act.wait_ge(s_fw, 128 * g + 64 * op[1] + 128)
                        split(1 - op[1], op[2], None)

            over_pairs(act, pairs)

        @block.vector
        def _(dve):
            dve.nop().then_inc(s_res, 1)
            count = Count(s_dve)
            for b in range(BATCH):
                dve.wait_ge(s_x[b], 16)
                normalise(dve, count, res[:, b * TOK_TILES:(b + 1) * TOK_TILES, :], norm, b * TOK_TILES, TOK_TILES,
                          s_var, s_pow, b + 1)

            def low(t):
                dve.wait_ge(s_xh, t + 1)
                cols = slice(t * P, (t + 1) * P)
                dve.tensor_tensor(xl[:, :, cols], ps[:, S_BANK + t % 2, :].rearrange("p (c n) -> p c n", c=KC),
                                  xh[:, :, cols].bitcast(F32), ALU.subtract).then_inc(s_xl, 1)

            for t in range(TILES):
                if t >= 2:
                    dve.wait_ge(s_xt, t - 1)
                dve.tensor_scalar(probs[:, t % 2, :], res[:, t, :], mv[:, t, 0:1], rstd[:, t:t + 1],
                                  ALU.subtract, ALU.mult).then_inc(s_xn, 1)
                if t >= 1:
                    low(t - 1)
            low(TILES - 1)

            def split(dst, hi, raw, value):
                dve.wait_ge(s_wh, value)
                dve.tensor_tensor(dst, raw, hi.bitcast(F32), ALU.subtract).then_inc(s_wl, 1)

            def split_in(n, value):
                split(wl[:, :, columns(n)], wh[:, :, columns(n)], w_raw[:, :, columns(n)], value)

            for n in range(NPROJ):
                split_in(n, n + 1)

            def maxima(g, u):
                w = (u % TOK_TILES + 1) * P
                dve.wait_ge(s_s, N_UNIT * g + u + 1)
                dve.tensor_reduce(nmax[:, u % 4:u % 4 + 1], ps[:, S_BANK + u % 2, 0:w], AX_X, ALU.max,
                                  negate=True).then_inc(s_max, 1)

            def weigh(g, u, count):
                i, w = u % 4, (u % TOK_TILES + 1) * P
                dve.wait_ge(s_exp, N_UNIT * g + u + 2)
                count.seal(dve, dve.reciprocal(rinv[:, i:i + 1], rsum[:, i:i + 1]))
                dve.tensor_scalar(probs[:, i, 0:w], probs[:, i, 0:w], rinv[:, i:i + 1], None, ALU.mult)\
                   .then_inc(s_pn, 1)

            maxima(0, 0)

            def group(g, last, base):
                count = Count(s_dve, base)
                weighed = 0
                for op, c, t, k in walk(last):
                    if op[0] == "score":
                        maxima(g, op[1])
                    if op[0] == "score" or (op[0] == "turn" and op[1] >= weighed):
                        weigh(g, weighed, count)
                        weighed += 1
                    elif op[0] == "split_out":
                        split(wol[:, op[1], :], woh[:, op[1], :], wo_raw[:, op[1], :],
                              N_SPLIT * g + NPROJ + op[1] + 1)
                    elif op[0] == "split_in":
                        split_in(op[1], N_SPLIT * g + N_SPLIT + op[1] + 1)
                    elif op[0] == "pv":
                        dve.wait_ge(s_ah, N_HEAD * g + op[1] + 1)
                        dve.tensor_tensor(al[:, op[1] % QPG, :], ps[:, O_BANK + op[1] % 2, :],
                                          ah[:, op[1] % QPG, :].bitcast(F32), ALU.subtract).then_inc(s_al, 1)
                    elif op[0] == "out":
                        tile = op[2] * TOK_TILES + op[1]
                        dve.wait_ge(s_g, NPROJ + N_CHAIN * g + c + 1)
                        dve.tensor_tensor(res[:, tile, :], ps[:, G_BANK + c % 2, :], res[:, tile, :], ALU.add)\
                           .then_inc(s_res, 1)
                return count.n

            base = count.n
            with dve.Fori(0, GROUPS - 1) as g:
                used = group(g, False, N_UNIT * g + base)
            assert used == N_UNIT
            group(GROUPS - 1, True, N_UNIT * (GROUPS - 1) + base)
            if phases == "A":
                return

            res_b = res[:, :, :].rearrange("p (b t) c -> p b t c", b=BATCH)
            count = Count(s_dve, N_UNIT * GROUPS + base)

            def queries(b):
                for t in range(TOK_TILES):
                    dve.tensor_scalar(xn[:, t, :], res_b[:, b, t, :], mv[:, t, 0:1], rstd[:, t:t + 1],
                                      ALU.subtract, ALU.mult).then_inc(s_xn2, 1)

            dve.wait_ge(s_res, TILES * GROUPS + 1)
            normalise(dve, count, res_b[:, 0], norm, 0, TOK_TILES, s_var, s_pow, BATCH + 1)
            queries(0)

            def maximum(m, slot, u):
                h, i = u // TOK_TILES, u % TOK_TILES
                dve.wait_ge(s_xs, 16 * m + u + 1)
                dve.tensor_reduce(xmax[:, slot, i, h:h + 1], ps[:, XS + u % 2, :], AX_X, ALU.max,
                                  negate=True).then_inc(s_xmax, 1)

            for u in range(XG * TOK_TILES):
                maximum(0, 0, u)
            counts = [count]

            def cross(b, kv, steps):
                m = KV * b + kv
                if kv == 0 and not (isinstance(b, int) and b in (0, BATCH)):
                    counts.append(Count(s_dve, counts[0].start + counts[0].n + X_MARKS * b - X_MARKS))
                count = counts[-1]
                if not (isinstance(b, int) and b >= BATCH - 1):
                    if kv == 1:
                        normalise(dve, count, res_b[:, b + 1], norm, 0, TOK_TILES, s_var, s_pow, BATCH + 2 + b)
                    if kv == KV - 3:
                        dve.wait_ge(s_xq, KV * TOK_TILES * b + KV * TOK_TILES)
                        queries(b + 1)
                for op in steps:
                    if op[0] == "s":
                        maximum(m + 1, (kv + 1) % 2, op[1])
                    elif op[:2] == ("t", "o"):
                        dve.wait_ge(s_ot, m - 1)
                        o = ps[:, XT, :].rearrange("p (t h d) -> p t h d", t=TOK_TILES, h=XG)
                        count.seal(dve, dve.reciprocal(xrec[:, :, :], o[:, :, :, XD]))
                        for t in range(TOK_TILES):
                            ready = count.mark(dve.tensor_tensor(
                                xo[:, t], o[:, t, :, 0:XD],
                                xrec[:, t, :].unsqueeze(2).to_broadcast([P, XG, XD]), ALU.mult))
                        dve.wait_ge(s_dve, ready)
                        at = ((kv - 2) % KV) * XG * XD
                        dst = res_b[:, b - (kv < 2), :, at:at + XG * XD]
                        dve.tensor_tensor(dst, xo[:, :, :, :].rearrange("p t h d -> p t (h d)"), dst, ALU.add)\
                            .then_inc(s_to, 1)

            over_items(cross)(dve)
            assert counts[1].n == X_MARKS
            if phases == "AB":
                return

            dve.nop().then_inc(s_yr, 1)
            dve.nop().then_inc(s_yr, 1)
            count = counts[-1]
            dve.wait_ge(s_to, ITEMS)
            for b in range(BATCH):
                normalise(dve, count, res_b[:, b], norm, b * TOK_TILES, TOK_TILES, s_var, s_pow, 2 * BATCH + b + 1)

            def low(t):
                dve.wait_ge(s_fh, t + 1)
                cols = slice(t * P, (t + 1) * P)
                dve.tensor_tensor(fl[:, :, cols], ps[:, H1 + t % 2, :].rearrange("p (c n) -> p c n", c=KC),
                                  fh[:, :, cols].bitcast(F32), ALU.subtract).then_inc(s_fl, 1)

            for t in range(TILES):
                if t >= 2:
                    dve.wait_ge(s_ft, t - 1)
                dve.tensor_scalar(fn[:, t % 2, :], res[:, t, :], mv[:, t, 0:1], rstd[:, t:t + 1],
                                  ALU.subtract, ALU.mult).then_inc(s_fn, 1)
                if t >= 1:
                    low(t - 1)
                if t == 0:
                    dve.wait_ge(s_gs, 1)
                    dve.tensor_tensor(gate_s[:, :, EXPERTS:], gate_raw[:, :, :], gate_s[:, :, 0:EXPERTS].bitcast(F32),
                                      ALU.subtract).then_inc(s_gs, 1)
            low(TILES - 1)

            def split(par, n, value):
                dve.wait_ge(s_wa, value)
                dst, hi, raw = ((w12l[:, par, :, n, :], w12h[:, par, :, n, :], w12_raw[:, :, n, :]) if n < 2 else
                                (w3l[:, par, :, :], w3h[:, par, :, :], w3_raw[:, :, :]))
                dve.tensor_tensor(dst, raw, hi.bitcast(F32), ALU.subtract).then_inc(s_wb, 1)

            for n in range(3):
                split(0, n, n + 1 + (n == 2))

            def spread(t):
                return t.unsqueeze(2).to_broadcast([P, TILES, EXPERTS])

            dve.wait_ge(s_la, 1)
            count.seal(dve, dve.tensor_tensor(logit[:, :, :], gate_ps[:, :, 0:EXPERTS], glow[:, :, :], ALU.add))
            count.seal(dve, dve.tensor_reduce(gmax[:, :], logit[:, :, :], AX_X, ALU.max))
            dve.tensor_tensor(logit[:, :, :], logit[:, :, :], spread(gmax[:, :]), ALU.subtract).then_inc(s_lb, 1)
            dve.wait_ge(s_la, 2)
            count.seal(dve, dve.tensor_reduce(gmax[:, :], gprob[:, :, :], AX_X, ALU.add))
            count.seal(dve, dve.reciprocal(gmax[:, :], gmax[:, :]))
            count.seal(dve, dve.tensor_tensor(gprob[:, :, :], gprob[:, :, :], spread(gmax[:, :]), ALU.mult))
            for t in range(TILES):
                ready = count.mark(dve.max(top[:, t, :], gprob[:, t, :]))
            dve.wait_ge(s_dve, ready)
            for t in range(TILES):
                ready = count.mark(dve.max_index(top_i[:, t, :], top[:, t, :], gprob[:, t, :]))
            dve.wait_ge(s_dve, ready)
            count.seal(dve, dve.tensor_copy(top_f[:, :, 0:2], top_i[:, :, 0:2]))
            numbers = number[:, :].unsqueeze(1).to_broadcast([P, TILES, EXPERTS])
            dve.wait_ge(s_cst, 8 + EXPERTS + 1)
            for n in range(2):
                ready = count.mark(dve.tensor_tensor(pick[:, n], numbers, spread(top_f[:, :, n]), ALU.is_equal))
            dve.wait_ge(s_dve, ready)
            count.seal(dve, dve.tensor_tensor(pick[:, 0], pick[:, 0], pick[:, 1], ALU.add))
            count.seal(dve, dve.tensor_tensor(comb[:, :, 0:EXPERTS], gprob[:, :, :], pick[:, 0], ALU.mult))
            count.seal(dve, dve.tensor_copy(comb_h[:, :, :], comb[:, :, :]))
            count.seal(dve, dve.tensor_copy(parts[:, :, 0:KINDS], comb_h[:, :, :]))
            count.seal(dve, dve.tensor_tensor(comb[:, :, :], comb[:, :, :], comb_h[:, :, :], ALU.subtract))
            count.seal(dve, dve.tensor_copy(comb_m[:, :, :], comb[:, :, :]))
            count.seal(dve, dve.tensor_copy(parts[:, :, KINDS:2 * KINDS], comb_m[:, :, :]))
            dve.tensor_tensor(parts[:, :, 2 * KINDS:], comb[:, :, :], comb_m[:, :, :], ALU.subtract).then_inc(s_cp, 1)

            def gated(n, i):
                dve.wait_ge(s_si, n + 1)
                dve.wait_ge(s_h2, n + 1)
                dve.tensor_tensor(prod[:, i, :], ps[:, H2 + i, :], act_s[:, i, :], ALU.mult).then_inc(s_pr, 1)
                dve.wait_ge(s_pr, n + 1)
                if not (isinstance(n, int) and n < 2):
                    dve.wait_ge(s_hl, n - 1)
                dve.tensor_tensor(hid[:, i, :], ps[:, HC + i, :], prod[:, i, :], ALU.mult).then_inc(s_hd, 1)

            gated(0, 0)
            gated(1, 1)

            def pairs(g, last):
                for op in ffn_steps(False, last):
                    if op[0] == "h":
                        gated(4 * BATCH * g + 2 * op[1] + op[2], op[2])
                    elif op[0] == "y":
                        q, t = op[1:]
                        tile = q % BATCH * TOK_TILES + t
                        dve.wait_ge(s_y, 8 * BATCH * g + 4 * q + t + 1)
                        dve.tensor_tensor(res[:, tile, :], ps[:, HY + t % 2, :], res[:, tile, :], ALU.add)\
                            .then_inc(s_yr, 1)
                    else:
                        split(1 - op[1], op[2], 8 * g + 4 * op[1] + 4 + op[2] + 1 + (op[2] == 2))

            over_pairs(dve, pairs)


def kernel(x, ctx_512, L0_attn_weight_qkv, L0_attn_weight_proj, L0_ffn_gate_w, L0_ffn_w1, L0_ffn_w2, L0_ffn_w3,
           L0_ffn_sw1, L0_ffn_sw2, L0_ffn_sw3):
    import numpy as np
    import concourse.bacc as bacc
    from concourse.bass_utils import run_bass_kernel_spmd

    f32 = np.float32

    def rows(experts, shared):
        experts = np.asarray(experts)
        n = experts.shape[0] * experts.shape[1]
        all_rows = np.zeros((ROWS_PAD, HID), f32)
        all_rows[:n] = experts.reshape(n, HID)
        all_rows[n:ROWS] = np.asarray(shared)
        return all_rows

    kinds = np.zeros((PARTS, ROWS_PAD), np.dtype("bfloat16"))
    for part in range(3):
        for e in range(KINDS):
            kinds[part * KINDS + e, e * WIDE:(e + 1) * WIDE if e < EXPERTS else ROWS] = 1
    arrays = {
        "x": np.ascontiguousarray(x),
        "ctx": np.ascontiguousarray(ctx_512),
        "w_qkv_t": np.ascontiguousarray(np.asarray(L0_attn_weight_qkv).T),
        "w_proj_t": np.ascontiguousarray(np.asarray(L0_attn_weight_proj).T),
        "gate_t": np.ascontiguousarray(np.asarray(L0_ffn_gate_w).T),
        "w1_t": np.ascontiguousarray(rows(L0_ffn_w1, L0_ffn_sw1).T),
        "w2_t": np.ascontiguousarray(rows(L0_ffn_w2, L0_ffn_sw2).T),
        "w3_t": rows(np.asarray(L0_ffn_w3).transpose(0, 2, 1), np.asarray(L0_ffn_sw3).T),
        "kinds": kinds,
    }
    nc = bacc.Bacc("TRN2", target_bir_lowering=False, num_devices=1)
    args = [nc.dram_tensor(f"in_{n}", a.shape, mybir.dt.from_np(a.dtype), kind="ExternalInput").ap()
            for n, a in arrays.items()]
    out = nc.dram_tensor("out", (BATCH, SEQ, HID), F32, kind="ExternalOutput").ap()
    build(nc, *args, out, phases=PHASES)
    r = run_bass_kernel_spmd(nc, [{f"in_{n}": a for n, a in arrays.items()}], core_ids=[0])
    return r.results[0]["out"]
```

```python
from contextlib import ExitStack

import concourse.bass as bass
from concourse import mybir

P = 128
ALU = mybir.AluOpType
ACT = mybir.ActivationFunctionType
AX_X = mybir.AxisListType.X
F32 = mybir.dt.float32
F32R = mybir.dt.float32r
BF16 = mybir.dt.bfloat16

BATCH, SEQ, HID = 4, 512, 512
TOK_TILES = SEQ // P
TILES = BATCH * TOK_TILES
KC = HID // P
GROUPS, QPG, D = 4, 4, 128
NPROJ = QPG + 2
EPS = 1e-5
MASKED = -3.0e38
ATT_SCALE = float(D) ** -0.5

PROJ_ORDER = [QPG, QPG + 1, 0, 1, 2, 3]
UNITS = QPG * TOK_TILES


class Count:

    def __init__(self, sem, start=0):
        self.sem, self.start, self.n = sem, start, 0

    def mark(self, ins):
        ins.then_inc(self.sem, 1)
        self.n += 1
        return self.start + self.n

    def seal(self, eng, ins):
        eng.wait_ge(self.sem, self.mark(ins))

def side_work(b, last):
    plan = {6: ["k"], 7: ["v"], 8: ["q0"], 9: ["vt"], 10: ["q1"], 12: ["q2"], 14: ["q3"]}
    if b == BATCH - 1:
        if last:
            plan = {}
        else:
            plan[16], plan[17] = plan.pop(12), plan.pop(14)
        plan[18] = ["y0", "y1", "y2", "y3"]
    if b > 0:
        plan[2], plan[3], plan[4] = ["y0"], ["y1"], ["y2", "y3"]
    return plan


START_CROSS = ([(("moments",), (2, 6)), (("roots",), (2, 8)), (("queries",), (3, 2))]
               + [(("first_t", kind, which, item), (3, 5 + n // 2)) for n, (item, which, kind) in enumerate(
                   [(i, w, k) for i in range(2) for w in range(2) for k in "kq"][:-1])]
               + [(("first_s", u), (3, 9 + u // 2)) for u in range(16)])


def attention_steps(last):
    ops = []
    for b in range(BATCH):
        plan = side_work(b, last)
        for s in range(UNITS + (3 if b == BATCH - 1 else 0)):
            start = [op for op, at in START_CROSS if at == (b, s)] if last else []
            ops += start[0:1]
            score, done = b * UNITS + s + 1, b * UNITS + s - 1
            if s < UNITS and score < BATCH * UNITS + (not last):
                ops.append(("score", score))
            if b == 0 and s < QPG:
                ops.append(("split_out", s))
            if b == BATCH - 1 and s < NPROJ and not last:
                ops.append(("split_in", s))
            ops += [("chain", c, (b + 1) % BATCH) for c in plan.get(s, []) if c[0] != "y"]
            if s <= UNITS + 1 and done >= TOK_TILES and done % TOK_TILES == 0:
                ops.append(("pv", done // TOK_TILES - 1))
            if s <= UNITS and done >= 0:
                ops.append(("turn", done))
            ops += [("out", int(c[1]), b if s > UNITS else b - 1) for c in plan.get(s, []) if c[0] == "y"]
            ops += start[1:]
    return ops


PROLOGUE = [(0, ()), (1, ()), (2, range(4, 8)), (3, ()), (4, range(8, 12)), (5, range(12, 16))]


def is_chain(op):
    return op[0] == "out" or (op[0] == "chain" and op[1] != "vt")


def is_turn(op):
    return op[0] == "turn" or (op[0] == "chain" and op[1] == "vt")


STEPS = {last: attention_steps(last) for last in (False, True)}
N_CHAIN = sum(map(is_chain, STEPS[False]))
N_TURN = sum(map(is_turn, STEPS[False]))
N_UNIT, N_HEAD, N_QKV, N_SPLIT = BATCH * UNITS, BATCH * QPG, BATCH * NPROJ, NPROJ + QPG
assert N_CHAIN % 2 == 0 and N_TURN % 2 == 0 and N_HEAD % 2 == 0


def walk(last):
    c = t = k = 0
    for op in STEPS[last]:
        yield op, c, t, k
        c += is_chain(op)
        t += is_turn(op)
        k += is_chain(op) and op[0] == "chain"


def piece_of(name):
    return {"k": 0, "v": 1}[name] if name in "kv" else 2 + int(name[1:])


def columns(piece):
    p = PROJ_ORDER[piece]
    return slice(p * P, (p + 1) * P)


def unit_of(u):
    return u // UNITS % BATCH, u // TOK_TILES % QPG, u % TOK_TILES


def products(pe, dst, pairs):
    for n, (lhs, rhs) in enumerate(pairs):
        last = pe.matmul(dst, lhs, rhs, start=(n == 0), stop=(n == len(pairs) - 1))
    return last


def turned(pe, dst, src, ident):
    return pe.matmul(dst, src, ident, start=True, stop=True, is_transpose=True)


def moments(eng, count, src, st, first, n, s_var):
    tiles = slice(first, first + n)
    for t in range(n):
        ready = count.mark(eng.bn_stats(st["stats"][:, first + t, :], src[:, t, :]))
    eng.wait_ge(count.sem, ready)
    count.mark(eng.memset(st["nt"][:, tiles], 0.0))
    for t in range(first, first + n):
        ready = count.mark(eng.bn_aggr(st["mv"][:, t, :], st["stats"][:, t, :]))
    eng.wait_ge(count.sem, ready)
    eng.tensor_scalar(st["ve"][:, tiles], st["mv"][:, tiles, 1], EPS, None, ALU.add).then_inc(s_var, 1)


def roots(eng, count, st, first, n, s_pow, pow_value):
    tiles = slice(first, first + n)
    ve, rstd, nt = st["ve"][:, tiles], st["rstd"][:, tiles], st["nt"][:, tiles]
    eng.wait_ge(s_pow, pow_value)
    count.seal(eng, eng.tensor_tensor(nt, rstd, rstd, ALU.mult))
    count.seal(eng, eng.tensor_tensor(nt, nt, ve, ALU.mult))
    count.seal(eng, eng.tensor_scalar(nt, nt, -0.5, 1.5, ALU.mult, ALU.add))
    count.seal(eng, eng.tensor_tensor(rstd, rstd, nt, ALU.mult))


NORM_MARKS = 2 * TOK_TILES + 5

RESULT_MARKS = 1 + TOK_TILES

KV, XG, XD = 8, 4, 16
X_SCALE = XD ** -0.5
SLOT = 64
X_ONE = 3 * XD
X_MARKS = KV * RESULT_MARKS + NORM_MARKS
ITEMS = BATCH * KV
VW = 32


def cross_steps(kv, m_left):
    turns = {0: ("k", 0, 2), 1: ("q", 0, 2), 2: ("m", 1, 0), 3: ("k", 1, 2), 4: ("o", 0, -2), 6: ("m", 0, 1),
             7: ("q", 1, 2)}
    ops = []
    s_units = iter(range(XG * TOK_TILES))
    for k in range(8):
        units = [("s", next(s_units)) for _ in range(1 if k % 2 else 3)] if m_left >= 1 else []
        if k % 2 == 0:
            ops += units[0:1]
            units = units[1:]
        if m_left >= 0:
            ops.append(("st", k))
        ops += units[0:1]
        if k in turns and (m_left >= turns[k][2] if turns[k][0] != "o" else kv >= 2):
            ops.append(("t",) + turns[k])
        ops += units[1:]
        if kv >= 1 and m_left >= -1 and k % 2:
            ops.append(("pv", k // 2))
    return ops


TA_START, TA_ITEM = 9, 6


EXPERTS, WIDE, SHARED = 8, 352, 704
ROWS = EXPERTS * WIDE + SHARED
PAIR = 2 * P
N_PAIR = 2 * (-(-ROWS // (2 * PAIR)))
ROWS_PAD = N_PAIR * PAIR
KINDS = EXPERTS + 1
PARTS = 3 * KINDS


def ffn_steps(last):
    ops = []
    for half in range(2):
        for ch in range(BATCH):
            q = half * BATCH + ch
            more = not (last and q == 2 * BATCH - 1)
            for i in range(2):
                if more:
                    ops.append(("h", q + 1, i))
                ops += [("y", q, 2 * i), ("y", q, 2 * i + 1)]
            if ch < 3 and not (last and half == 1):
                ops.append(("w", half, ch))
    return ops


def over_pairs(eng, body):
    with eng.Fori(0, N_PAIR // 2 - 1) as g:
        body(g, False)
    body(N_PAIR // 2 - 1, True)


def over_items(item):
    def batch(b, before, left):
        for kv in range(KV):
            item(b, kv, cross_steps(before + kv, left - kv))

    def run(eng):
        batch(0, 0, ITEMS)
        with eng.Fori(1, BATCH - 1) as b:
            batch(b, KV, ITEMS)
        batch(BATCH - 1, KV, KV - 1)
        for kv in range(2):
            item(BATCH, kv, cross_steps(KV, -1 - kv))
    return run


def build(nc, x, ctx_in, w_qkv_t, w_proj_t, gate_t, w1_t, w2_t, w3_t, kinds, out):
    x_v = x.rearrange("b (t p) c -> b p t c", p=P)
    ctx_v = ctx_in.rearrange("b (t p) c -> b p t c", p=P)
    w1_v = w1_t.rearrange("(c p) (g n) -> g p c n", p=P, g=N_PAIR)
    w2_v = w2_t.rearrange("(c p) (g n) -> g p c n", p=P, g=N_PAIR)
    w3_v = w3_t.rearrange("(g i p) n -> g p i n", p=P, g=N_PAIR)
    kinds_v = kinds.rearrange("k (g n) -> g k n", g=N_PAIR)
    gate_v = gate_t.rearrange("(c p) e -> p c e", p=P)
    out_v = out.rearrange("b (t p) c -> b p t c", p=P)
    w_v = w_qkv_t.rearrange("(c p) (g n) -> g p c n", p=P, g=GROUPS)
    wo_v = w_proj_t.rearrange("(g h p) n -> g p h n", p=P, g=GROUPS)

    with ExitStack() as whole:
        def sem(name):
            return whole.enter_context(nc.semaphore(name))

        def keep(name, shape, dt=F32):
            return whole.enter_context(nc.sbuf_tensor(name, shape, dt))

        ps = whole.enter_context(nc.psum_tensor("ps", [P, 8, 512], F32))
        res = keep("res", [P, TILES, HID])
        ident = keep("ident", [P, P])
        norm = {n: keep(n, [P, TILES] + w) for n, w in (("stats", [6]), ("mv", [2]), ("ve", []), ("rstd", []),
                                                        ("nt", []))}
        mv, rstd = norm["mv"], norm["rstd"]
        ones = keep("ones", [P, 1])
        half = keep("half", [P, TOK_TILES])

        s_x = [sem(f"s_x{b}") for b in range(BATCH)]
        s_cst = sem("s_cst")
        s_dve = sem("s_dve")
        s_var = sem("s_var")
        s_pow = sem("s_pow")
        s_xn = sem("s_xn")
        s_xt = sem("s_xt")
        s_xh = sem("s_xh")
        s_xl = sem("s_xl")
        s_out = sem("s_out")

        s_w = sem("s_w")
        s_wh = sem("s_wh")
        s_wl = sem("s_wl")
        s_s = sem("s_s")
        s_max = sem("s_max")
        s_exp = sem("s_exp")
        s_pn = sem("s_pn")
        s_t = sem("s_t")
        s_te = sem("s_te")
        s_pv = sem("s_pv")
        s_ah = sem("s_ah")
        s_al = sem("s_al")
        s_g = sem("s_g")
        s_q = sem("s_q")
        s_res = sem("s_res")
        S_BANK, T_BANK, O_BANK, G_BANK = 0, 2, 4, 6

        s_ctx = sem("s_ctx")
        s_pc = sem("s_pc")
        s_px = sem("s_px")
        s_pm = sem("s_pm")
        s_kc = sem("s_kc")
        s_xq = sem("s_xq")
        s_vx = sem("s_vx")
        s_xn2 = sem("s_xn2")
        s_xmax = sem("s_xmax")
        s_mq = sem("s_mq")
        s_kt = sem("s_kt")
        s_qt = sem("s_qt")
        s_mt = sem("s_mt")
        s_ot = sem("s_ot")
        s_ta = sem("s_ta")
        s_to = sem("s_to")
        s_xs = sem("s_xs")
        s_st = sem("s_st")
        s_xe = sem("s_xe")
        s_xpv = sem("s_xpv")
        s_oe = sem("s_oe")
        s_gw = sem("s_gw")
        s_gs = sem("s_gs")
        s_fn = sem("s_fn")
        s_ft = sem("s_ft")
        s_fh = sem("s_fh")
        s_fl = sem("s_fl")
        s_lg = sem("s_lg")
        s_la = sem("s_la")
        s_lb = sem("s_lb")
        s_cp = sem("s_cp")
        s_ct = sem("s_ct")
        s_ce = sem("s_ce")
        s_fw = sem("s_fw")
        s_wa = sem("s_wa")
        s_wb = sem("s_wb")
        s_h1 = sem("s_h1")
        s_h2 = sem("s_h2")
        s_si = sem("s_si")
        s_pr = sem("s_pr")
        s_hd = sem("s_hd")
        s_hh = sem("s_hh")
        s_hl = sem("s_hl")
        s_y = sem("s_y")
        s_yr = sem("s_yr")
        H1, H2, HC, HY = 0, 2, 4, 6
        XST, XS, XO, XT = 0, 4, 6, 7

        pa = ExitStack()

        def sba(name, shape, dt=F32):
            return pa.enter_context(nc.sbuf_tensor(name, shape, dt))

        xh = sba("xh", [P, KC, BATCH * SEQ], F32R)
        xl = sba("xl", [P, KC, BATCH * SEQ], F32R)
        w_raw = sba("w_raw", [P, KC, NPROJ * P])
        wo_raw = w_raw[:, :, :].rearrange("p c n -> p (c n)")[:, 0:QPG * HID].rearrange("p (h n) -> p h n", h=QPG)
        wh = sba("wh", [P, KC, NPROJ * P], F32R)
        wl = sba("wl", [P, KC, NPROJ * P], F32R)
        woh = sba("woh", [P, QPG, HID], F32R)
        wol = sba("wol", [P, QPG, HID], F32R)
        q_t = sba("q_t", [P, 2, QPG, SEQ])
        k_t = sba("k_t", [P, 2, SEQ])
        v_t = sba("v_t", [P, SEQ])
        v_s = sba("v_s", [P, 2, TOK_TILES, D])
        probs = sba("probs", [P, 4, SEQ])
        pt = sba("pt", [P, TOK_TILES, SEQ])
        ah = sba("ah", [P, QPG, SEQ], F32R)
        al = sba("al", [P, QPG, SEQ], F32R)
        mask = sba("mask", [P, P], BF16)
        ident_b = sba("ident_b", [P, P], BF16)
        nmax = sba("nmax", [P, 4])
        rsum = sba("rsum", [P, 4])
        rinv = sba("rinv", [P, 4])
        pa.close()

        pb = ExitStack()

        def sbb(name, shape, dt=F32):
            return pb.enter_context(nc.sbuf_tensor(name, shape, dt))

        xn = sbb("xn", [P, TOK_TILES, HID])
        kc = sbb("kc", [P, TOK_TILES, KV, 3 * SLOT])
        ctx_s = sbb("ctx_s", [P, TOK_TILES, KV * XD])
        xq = sbb("xq", [P, 4, TOK_TILES, XG, SLOT])
        vx = sbb("vx", [P, 4, TOK_TILES, VW])
        k3 = sbb("k3", [P, 4, 2, SEQ], F32R)
        q3 = sbb("q3", [P, 2, 2, SEQ], F32R)
        q3m = sbb("q3m", [P, 2, SEQ], F32R)
        o_t = sbb("o_t", [P, 2, SEQ])
        xmax = sbb("xmax", [P, 2, TOK_TILES, XG])
        xrec = sbb("xrec", [P, TOK_TILES, XG])
        xo = sbb("xo", [P, TOK_TILES, XG, XD])
        xp = sbb("xp", [P, 2, XG, TOK_TILES, SEQ])
        pb.close()

        pc = ExitStack()

        def sbc(name, shape, dt=F32):
            return pc.enter_context(nc.sbuf_tensor(name, shape, dt))

        fh = sbc("fh", [P, KC, BATCH * SEQ], F32R)
        fl = sbc("fl", [P, KC, BATCH * SEQ], F32R)
        fn = sbc("fn", [P, 2, HID])
        w12_raw = sbc("w12_raw", [P, KC, 2, PAIR])
        w3_raw = sbc("w3_raw", [P, 2, HID])
        kind_raw = sbc("kind_raw", [PARTS, PAIR], BF16)
        w12h = sbc("w12h", [P, 2, KC, 2, PAIR], F32R)
        w12l = sbc("w12l", [P, 2, KC, 2, PAIR], F32R)
        w3h = sbc("w3h", [P, 2, 2, HID], F32R)
        w3l = sbc("w3l", [P, 2, 2, HID], F32R)
        kind_s = sbc("kind_s", [PARTS, 2, PAIR], BF16)
        comb_t = sbc("comb_t", [PARTS, BATCH * SEQ], BF16)
        hidden_s = sbc("hidden_s", [P, 3, 2, SEQ])
        act_s, prod, hid = (hidden_s[:, n] for n in range(3))
        hh = sbc("hh", [P, 2, 2, SEQ], F32R)
        hl = sbc("hl", [P, 2, 2, SEQ], F32R)
        gate_raw = sbc("gate_raw", [P, KC, EXPERTS])
        gate_s = sbc("gate_s", [P, KC, 2 * EXPERTS], F32R)
        glow = sbc("glow", [P, TILES, EXPERTS])
        logit = sbc("logit", [P, TILES, EXPERTS])
        gprob = sbc("gprob", [P, TILES, EXPERTS])
        gmax = sbc("gmax", [P, TILES])
        top = sbc("top", [P, TILES, 8])
        top_i = sbc("top_i", [P, TILES, 8], mybir.dt.uint32)
        top_f = sbc("top_f", [P, TILES, 8])
        number = sbc("number", [P, EXPERTS])
        pick = sbc("pick", [P, 2, TILES, EXPERTS])
        comb = sbc("comb", [P, TILES, KINDS])
        comb_h = sbc("comb_h", [P, TILES, KINDS], BF16)
        comb_m = sbc("comb_m", [P, TILES, KINDS], BF16)
        parts = sbc("parts", [P, TILES, PARTS])
        pc.close()

        by_expert = hidden_s[0:2 * EXPERTS, 1:3].rearrange("p a b n -> p (a b n)")
        gate_ps = ps[:, HY + 1, 0:2 * EXPERTS * TILES].rearrange("p (t e) -> p t e", t=TILES)
        block = whole.enter_context(nc.Block())

        @block.sync
        def _(sp):
            for b in range(BATCH):
                sp.dma_start(res[:, b * TOK_TILES:(b + 1) * TOK_TILES, :], x_v[b]).then_inc(s_x[b], 16)
                if b == 0:
                    sp.dma_start(w_raw[:, :, :], w_v[0]).then_inc(s_w, 16)
            sp.wait_ge(s_wl, NPROJ)
            sp.dma_start(wo_raw, wo_v[0]).then_inc(s_w, 16)
            with sp.Fori(0, GROUPS - 1) as g:
                sp.wait_ge(s_wl, N_SPLIT * g + N_SPLIT)
                sp.dma_start(w_raw[:, :, :], w_v[g + 1]).then_inc(s_w, 16)
                sp.wait_ge(s_wl, N_SPLIT * g + N_SPLIT + NPROJ)
                sp.dma_start(wo_raw, wo_v[g + 1]).then_inc(s_w, 16)
            sp.wait_ge(s_q, N_QKV * GROUPS)
            sp.dma_start(ctx_s[:, :, :], ctx_v[0]).then_inc(s_ctx, 16)
            with sp.Fori(0, BATCH - 1) as b:
                sp.wait_ge(s_kc, TOK_TILES * b + TOK_TILES)
                sp.dma_start(ctx_s[:, :, :], ctx_v[b + 1]).then_inc(s_ctx, 16)
            def load_pair(g):
                sp.dma_start(w12_raw[:, :, 0, :], w1_v[g]).then_inc(s_fw, 16)
                sp.dma_start(w12_raw[:, :, 1, :], w2_v[g]).then_inc(s_fw, 16)
                sp.dma_start(w3_raw[:, :, :], w3_v[g]).then_inc(s_fw, 16)
                sp.dma_start(kind_raw[:, :], kinds_v[g]).then_inc(s_fw, 16)

            sp.wait_ge(s_xpv, ITEMS)
            load_pair(0)
            sp.dma_start(gate_raw[:, :, :], gate_v).then_inc(s_gw, 16)
            with sp.Fori(0, N_PAIR - 1) as g:
                sp.wait_ge(s_wb, 3 * g + 3)
                load_pair(g + 1)
            for b in range(BATCH):
                sp.wait_ge(s_yr, 2 + TILES * (N_PAIR - 1) + (b + 1) * TOK_TILES)
                sp.dma_start(out_v[b], res[:, b * TOK_TILES:(b + 1) * TOK_TILES, :]).then_inc(s_out, 16)
            sp.wait_ge(s_out, 16 * BATCH)

        @block.gpsimd
        def _(pool):
            pool.memset(ident[:, :], 0.0).then_inc(s_cst, 1)
            pool.memset(ident_b[:, :], 0.0).then_inc(s_cst, 1)
            pool.memset(mask[:, :], 0.0).then_inc(s_cst, 1)
            pool.memset(half[:, :], -0.5).then_inc(s_cst, 1)
            pool.memset(ones[:, :], 1.0).then_inc(s_cst, 1)
            pool.wait_ge(s_cst, 5)
            for t in (ident, ident_b):
                pool.affine_select(out=t[:, :], in_=t[:, :], compare_op=ALU.not_equal, fill=1.0, base=0,
                                   pattern=[[-1, P]], channel_multiplier=1).then_inc(s_cst, 1)
            pool.affine_select(out=mask[:, :], in_=mask[:, :], compare_op=ALU.is_ge, fill=MASKED, base=0,
                               pattern=[[-1, P]], channel_multiplier=1).then_inc(s_cst, 1)

            def power(b, value):
                tiles = slice(b * TOK_TILES, (b + 1) * TOK_TILES)
                pool.wait_ge(s_var, value)
                pool.tensor_tensor(rstd[:, tiles], norm["ve"][:, tiles], half[:, :], ALU.pow).then_inc(s_pow, 1)

            for b in range(BATCH):
                power(b, b + 1)

            power(0, BATCH + 1)
            pool.wait_ge(s_q, N_QKV * GROUPS)
            pool.memset(kc[:, :, :, :], 0.0).then_inc(s_pc, 1)
            pool.memset(xq[:, :, :, :, :], 0.0).then_inc(s_pc, 1)
            pool.memset(vx[:, :, :, :], 0.0).then_inc(s_pc, 1)
            pool.wait_ge(s_pc, 3)
            pool.memset(kc[:, :, :, SLOT + X_ONE:SLOT + X_ONE + 2], 1.0).then_inc(s_pc, 1)
            pool.memset(vx[:, :, :, XD:XD + 1], 1.0).then_inc(s_pc, 1)
            pool.wait_ge(s_pc, 5)
            ctx_h = ctx_s[:, :, :].rearrange("p t (k d) -> p t k d", k=KV)

            def high(dst, src, shape):
                one = ones[:, :].unsqueeze(2).to_broadcast([P] + list(shape))
                return pool.tensor_tensor(dst.bitcast(F32R), src, one, ALU.mult)

            def build_keys(b):
                pool.wait_ge(s_ctx, 16 * b + 16)
                at = kc[:, :, :, SLOT:2 * SLOT]
                for i in range(TOK_TILES):
                    for n in (0, 2):
                        high(at[:, i, :, n * XD:(n + 1) * XD], ctx_h[:, i], (KV, XD)).then_inc(s_pc, 1)
                pool.wait_ge(s_pc, 5 + 8 * b + 8)
                for i in range(TOK_TILES):
                    pool.tensor_tensor(at[:, i, :, XD:2 * XD].bitcast(F32R), ctx_h[:, i], at[:, i, :, 0:XD],
                                       ALU.subtract).then_inc(s_kc, 1)

            def build_queries(slot, kv, value):
                src = xn[:, :, kv * XG * XD:(kv + 1) * XG * XD].rearrange("p t (h d) -> p t h d", h=XG)
                for n in (0, 1):
                    for i in range(TOK_TILES):
                        high(xq[:, slot, i, :, n * XD:(n + 1) * XD], src[:, i], (XG, XD)).then_inc(s_px, 1)
                pool.memset(xq[:, slot, :, :, X_ONE:X_ONE + 2], 0.0).then_inc(s_px, 1)
                pool.wait_ge(s_px, value)
                for i in range(TOK_TILES):
                    pool.tensor_tensor(xq[:, slot, i, :, 2 * XD:3 * XD].bitcast(F32R), src[:, i],
                                       xq[:, slot, i, :, 0:XD], ALU.subtract).then_inc(s_xq, 1)

            def build_values(kv):
                pool.tensor_tensor(vx[:, kv % 4, :, 0:XD], kc[:, :, kv, SLOT:SLOT + XD],
                                   kc[:, :, kv, SLOT + XD:SLOT + 2 * XD], ALU.add).then_inc(s_vx, 1)

            def put_maxima(slot, pair, units, value):
                pool.wait_ge(s_xmax, units)
                heads = slice(2 * pair, 2 * pair + 2)
                high(xq[:, slot, :, heads, X_ONE], xmax[:, slot % 2, :, heads], (TOK_TILES, 2)).then_inc(s_pm, 1)
                pool.wait_ge(s_pm, value)
                pool.tensor_tensor(xq[:, slot, :, heads, X_ONE + 1].bitcast(F32R), xmax[:, slot % 2, :, heads],
                                   xq[:, slot, :, heads, X_ONE], ALU.subtract).then_inc(s_mq, 1)

            build_keys(0)
            pool.wait_ge(s_kc, TOK_TILES)
            build_values(0)
            build_values(1)
            pool.wait_ge(s_xn2, TOK_TILES)
            for kv in range(3):
                build_queries(kv, kv, 9 * kv + 9)
            put_maxima(0, 0, 2 * TOK_TILES, 1)
            put_maxima(0, 1, 4 * TOK_TILES, 2)

            def cross(b, first, last):
                for kv in range(KV):
                    m = KV * b + kv
                    if not (last and kv >= KV - 3):
                        if kv == KV - 3:
                            pool.wait_ge(s_xn2, TOK_TILES * b + 2 * TOK_TILES)
                        if not (first and kv == 0):
                            pool.wait_ge(s_mt, 2 * m)
                        build_queries((kv + 3) % 4, (kv + 3) % KV, 9 * m + 36)
                    if kv == 1 and not last:
                        power_next(b)
                    if not (last and kv >= KV - 2):
                        if kv == KV - 2:
                            pool.wait_ge(s_kc, TOK_TILES * b + 2 * TOK_TILES)
                        if not (first and kv < 2):
                            pool.wait_ge(s_xpv, m - 1)
                        build_values((kv + 2) % KV)
                    if kv == KV - 3 and not last:
                        pool.wait_ge(s_kt, 2 * m + 6)
                        pool.wait_ge(s_vx, m + 3)
                        build_keys(b + 1)
                    if last and 3 <= kv < 6:
                        power(kv - 3, 2 * BATCH + kv - 2)
                    if not (last and kv == KV - 1):
                        put_maxima((kv + 1) % 4, 0, 16 * m + 24, 2 * m + 3)
                        put_maxima((kv + 1) % 4, 1, 16 * m + 32, 2 * m + 4)

            def power_next(b):
                tiles = slice(0, TOK_TILES)
                pool.wait_ge(s_var, BATCH + b + 2)
                pool.tensor_tensor(rstd[:, tiles], norm["ve"][:, tiles], half[:, :], ALU.pow).then_inc(s_pow, 1)

            cross(0, True, False)
            with pool.Fori(1, BATCH - 1) as b:
                cross(b, False, False)
            cross(BATCH - 1, False, True)

            pool.wait_ge(s_to, ITEMS)
            for e in range(EXPERTS):
                pool.memset(number[:, e:e + 1], float(e)).then_inc(s_cst, 1)
            pool.memset(comb[:, :, EXPERTS:KINDS], 1.0).then_inc(s_cst, 1)
            power(BATCH - 1, 3 * BATCH)

            def low(n, slot, i):
                pool.wait_ge(s_hh, n + 1)
                pool.tensor_tensor(hl[:, slot, i, :], hid[:, i, :], hh[:, slot, i, :].bitcast(F32), ALU.subtract)\
                    .then_inc(s_hl, 1)

            low(0, 0, 0)
            low(1, 0, 1)

            def pairs(g, last):
                for op in ffn_steps(last):
                    if op[0] == "h":
                        low(4 * BATCH * g + 2 * op[1] + op[2], op[1] % 2, op[2])

            over_pairs(pool, pairs)

        @block.tensor
        def _(pe):
            pe.wait_ge(s_cst, 8)
            def turn_tile(t):
                pe.wait_ge(s_xn, t + 1)
                if t >= 4:
                    pe.wait_ge(s_xl, t - 3)
                for c in range(KC):
                    last = turned(pe, ps[:, S_BANK + t % 4, c * P:(c + 1) * P],
                                  probs[:, t % 4, c * P:(c + 1) * P], ident[:, :])
                last.then_inc(s_xt, 1)

            for t in range(TOK_TILES):
                turn_tile(t)

            def project(piece, b, bank):
                toks = slice(b * SEQ, (b + 1) * SEQ)
                products(pe, ps[:, G_BANK + bank, :],
                         [(w[:, c, columns(piece)], xx[:, c, toks])
                          for w, xx in ((wh, xh), (wl, xh), (wh, xl)) for c in range(KC)]).then_inc(s_g, 1)

            def turn_v(bank):
                for t in range(TOK_TILES):
                    last = turned(pe, ps[:, T_BANK + bank, t * P:(t + 1) * P], v_t[:, t * P:(t + 1) * P], ident[:, :])
                last.then_inc(s_t, 1)

            def scores(u):
                b, h, i = unit_of(u)
                w = (i + 1) * P
                pe.matmul(ps[:, S_BANK + u % 2, i * P:w], ident_b[:, :], mask[:, :], start=True, stop=True)
                pe.matmul(ps[:, S_BANK + u % 2, 0:w], q_t[:, b % 2, h, i * P:w], k_t[:, b % 2, 0:w],
                          start=False, stop=True, skip_group_check=True).then_inc(s_s, 1)

            pe.wait_ge(s_xl, TOK_TILES)
            for n, behind in PROLOGUE:
                pe.wait_ge(s_wl, n + 1)
                if n >= 2:
                    pe.wait_ge(s_q, n - 1)
                project(n, 0, n % 2)
                for t in behind:
                    turn_tile(t)
            pe.wait_ge(s_xl, TILES)
            pe.wait_ge(s_q, 2)
            turn_v(0)
            pe.wait_ge(s_q, 3)
            scores(0)

            def chain_taken(g, last, c):
                if c < 2:
                    pe.wait_ge(s_q, N_QKV * g + NPROJ)
                    pe.wait_ge(s_res, TILES * g + 1)
                    return
                before = [(op, k) for op, n, t, k in walk(last) if is_chain(op) and n == c - 2][0]
                if before[0][0] == "out":
                    pe.wait_ge(s_res, TILES * g + before[0][2] * TOK_TILES + before[0][1] + 2)
                else:
                    pe.wait_ge(s_q, N_QKV * g + NPROJ + before[1] + 1)

            def turn_first(kind, which, item, n):
                if kind == "k":
                    pe.wait_ge(s_kc, TOK_TILES)
                elif kind == "q":
                    pe.wait_ge(s_xq, TOK_TILES * (item + 1))
                else:
                    pe.wait_ge(s_mq, 1)
                if n:
                    pe.wait_ge(s_ta, n)
                for i in range(TOK_TILES):
                    src = kc[:, i, item, SLOT * (1 - which):SLOT * (3 - which)] if kind == "k" else \
                        xq[:, item, i, 2 * which:2 * which + 2, :].rearrange("p h c -> p (h c)")
                    ins = turned(pe, ps[:, XT, i * P:(i + 1) * P], src, ident[:, :])
                ins.then_inc({"k": s_kt, "q": s_qt, "m": s_mt}[kind], 1)

            def group(g, last):
                for op, c, t, k in walk(last):
                    if op[0] == "first_t":
                        n = 4 * op[3] + 2 * op[2] + (op[1] == "q")
                        if n == 0:
                            pe.wait_ge(s_res, TILES * g + (BATCH - 1) * TOK_TILES + 1)
                        turn_first(op[1], op[2], op[3], n)
                    elif op[0] == "first_s":
                        h, i = op[1] // TOK_TILES, op[1] % TOK_TILES
                        if op[1] == 0:
                            pe.wait_ge(s_ta, 7)
                        if op[1] >= 2:
                            pe.wait_ge(s_xmax, op[1] - 1)
                        pe.matmul(ps[:, G_BANK + op[1] % 2, :], q3[:, 0, h // 2, i * P:(i + 1) * P],
                                  k3[:, 0, h % 2, :], start=True, stop=True).then_inc(s_xs, 1)
                    elif op[0] == "score":
                        u = op[1]
                        if u % TOK_TILES == 0:
                            pe.wait_ge(s_q, N_QKV * g + NPROJ * (u // UNITS) + 3 + unit_of(u)[1])
                        pe.wait_ge(s_exp, N_UNIT * g + u)
                        scores(u)
                    elif op[0] == "turn":
                        pe.wait_ge(s_pn, N_UNIT * g + op[1] + 1)
                        pe.wait_ge(s_te, N_TURN * g + t + 1)
                        for j in range(op[1] % TOK_TILES + 1):
                            ins = turned(pe, ps[:, T_BANK + (1 + t) % 2, j * P:(j + 1) * P],
                                               probs[:, op[1] % 4, j * P:(j + 1) * P], ident[:, :])
                        ins.then_inc(s_t, 1)
                    elif op[0] == "pv":
                        b, h = op[1] // QPG, op[1] % QPG
                        pe.wait_ge(s_te, N_TURN * g + t + 2)
                        for j in reversed(range(TOK_TILES)):
                            ins = pe.matmul(ps[:, O_BANK + h % 2, j * P:], v_s[:, b % 2, j, :], pt[:, j, j * P:],
                                            start=(j == TOK_TILES - 1), stop=True, skip_group_check=True)
                        ins.then_inc(s_pv, 1)
                    elif op[0] == "out":
                        i, b = op[1:]
                        if i == 0:
                            pe.wait_ge(s_al, N_HEAD * g + QPG * (b + 1))
                            pe.wait_ge(s_wl, N_SPLIT * g + N_SPLIT)
                            if last and b == BATCH - 1:
                                pe.wait_ge(s_xmax, XG * TOK_TILES)
                        chain_taken(g, last, c)
                        toks = slice(i * P, (i + 1) * P)
                        products(pe, ps[:, G_BANK + c % 2, :],
                                 [(a[:, h, toks], w[:, h, :])
                                  for a, w in ((ah, woh), (ah, wol), (al, woh)) for h in range(QPG)]).then_inc(s_g, 1)
                    elif is_chain(op):
                        n = piece_of(op[1])
                        if op[2] == 0:
                            pe.wait_ge(s_wl, N_SPLIT * g + N_SPLIT + n + 1)
                        chain_taken(g, last, c)
                        project(n, op[2], c % 2)
                    elif op[0] == "chain":
                        pe.wait_ge(s_q, NPROJ + N_QKV * g + k - 1)
                        pe.wait_ge(s_te, N_TURN * g + t + 1)
                        turn_v((1 + t) % 2)

            with pe.Fori(0, GROUPS - 1) as g:
                group(g, False)
            group(GROUPS - 1, True)

            pe.wait_ge(s_res, GROUPS * TILES + 1)

            def cross(b, kv, steps):
                m = KV * b + kv
                now, ahead2 = ("st", 0) in steps, ("t", "k", 0, 2) in steps
                taken = TA_START + TA_ITEM * m
                if isinstance(m, int) and m == ITEMS - 1:
                    taken -= 4
                start = taken
                before_is_result = not now
                for op in steps:
                    if op[0] == "t":
                        kind, which, off = op[1:]
                        if before_is_result:
                            pe.wait_ge(s_to, m - 1 if kind != "o" else m - 2)
                        else:
                            pe.wait_ge(s_ta, taken)
                        before_is_result = kind == "o"
                        taken = taken + (kind != "o")
                        slot = (kv + off) % 4
                        if kind == "k":
                            pe.wait_ge(s_kc, TOK_TILES * (b + (kv + 2) // KV) + TOK_TILES)
                            for i in range(TOK_TILES):
                                src = kc[:, i, (kv + off) % KV, SLOT * (1 - which):SLOT * (3 - which)]
                                ins = turned(pe, ps[:, XT, i * P:(i + 1) * P], src, ident[:, :])
                            ins.then_inc(s_kt, 1)
                        elif kind in "qm":
                            if kind == "q":
                                pe.wait_ge(s_xq, TOK_TILES * m + 3 * TOK_TILES)
                            else:
                                pe.wait_ge(s_mq, 2 * (m + off) + which + 1)
                            for i in range(TOK_TILES):
                                src = xq[:, slot, i, 2 * which:2 * which + 2, :].rearrange("p h c -> p (h c)")
                                ins = turned(pe, ps[:, XT, i * P:(i + 1) * P], src, ident[:, :])
                            ins.then_inc(s_qt if kind == "q" else s_mt, 1)
                        else:
                            pe.wait_ge(s_oe, m - 1)
                            for i in range(TOK_TILES):
                                ins = turned(pe, ps[:, XT, i * P:(i + 1) * P], o_t[:, kv % 2, i * P:(i + 1) * P],
                                             ident[:, :])
                            ins.then_inc(s_ot, 1)
                    elif op[0] == "s":
                        h, i = op[1] // TOK_TILES, op[1] % TOK_TILES
                        if op[1] == 0:
                            pe.wait_ge(s_ta, start - 2)
                        if op[1] == 2 * TOK_TILES:
                            pe.wait_ge(s_ta, start)
                        pe.wait_ge(s_xmax, 16 * m + 16 + op[1] - 1)
                        pe.matmul(ps[:, XS + op[1] % 2, :], q3[:, (kv + 1) % 2, h // 2, i * P:(i + 1) * P],
                                  k3[:, (kv + 1) % 4, h % 2, :], start=True, stop=True).then_inc(s_xs, 1)
                    elif op[0] == "st":
                        h, pair = op[1] // 2, op[1] % 2
                        if op[1] == 0:
                            pe.wait_ge(s_ta, start - 1 if ("s", 0) in steps else start)
                        if op[1] == 4:
                            pe.wait_ge(s_ta, start + (3 if ahead2 else 1))
                        if not (isinstance(m, int) and 8 * m + op[1] < 2):
                            pe.wait_ge(s_xe, 8 * m + op[1] - 1)
                        for e in range(2):
                            t = 2 * pair + e
                            ins = pe.matmul(ps[:, XST + 2 * pair + e, :], k3[:, kv % 4, h % 2, t * P:(t + 1) * P],
                                            q3m[:, h // 2, :], start=True, stop=True)
                        ins.then_inc(s_st, 1)
                    else:
                        j, before = op[1], (kv - 1) % KV
                        if j == 0:
                            pe.wait_ge(s_vx, m)
                            if not (isinstance(m, int) and m < 2):
                                pe.wait_ge(s_oe, m - 1)
                        pe.wait_ge(s_xe, 8 * m - (1 if j < 2 else 0))
                        for h in range(XG):
                            ins = pe.matmul(ps[VW * h:VW * (h + 1), XO, :], vx[:, before % 4, j, :],
                                            xp[:, (kv - 1) % 2, h, j, :], start=(j == 0), stop=(j == TOK_TILES - 1),
                                            tile_position=(0, VW * h))
                        if j == TOK_TILES - 1:
                            ins.then_inc(s_xpv, 1)

            turn_first("m", 0, 0, 7)
            turn_first("q", 1, 1, 8)

            over_items(cross)(pe)

            pe.wait_ge(s_to, ITEMS)
            for t in range(TILES):
                pe.wait_ge(s_fn, t + 1)
                if t >= 2:
                    pe.wait_ge(s_fl, t - 1)
                for c in range(KC):
                    ins = turned(pe, ps[:, H1 + t % 2, c * P:(c + 1) * P], fn[:, t % 2, c * P:(c + 1) * P], ident[:, :])
                ins.then_inc(s_ft, 1)
            pe.wait_ge(s_gs, 2)
            pe.wait_ge(s_fl, TILES)
            for b in range(BATCH):
                if b == BATCH - 1:
                    pe.wait_ge(s_la, 1)
                toks = slice(b * SEQ, (b + 1) * SEQ)
                at = ps[0:2 * EXPERTS, HC + b % 3, :]
                for c in range(KC):
                    pe.matmul(at, gate_s[:, c, :], fh[:, c, toks], start=(c == 0), stop=True, skip_group_check=c > 0)
                for c in range(KC):
                    ins = pe.matmul(at[0:EXPERTS, :], gate_s[:, c, 0:EXPERTS], fl[:, c, toks], start=False, stop=True,
                                    skip_group_check=True)
                ins.then_inc(s_lg, 1)
            for t in range(TILES):
                if t % TOK_TILES == 0:
                    pe.wait_ge(s_la, t // TOK_TILES + 1)
                ins = turned(pe, ps[:, HY + 1, 2 * EXPERTS * t:2 * EXPERTS * (t + 1)], by_expert[:, t * P:(t + 1) * P],
                             ident[0:2 * EXPERTS, 0:2 * EXPERTS])
            ins.then_inc(s_lg, 1)

            def hidden(n, par, ch, i):
                rows = slice(i * P, (i + 1) * P)
                toks = slice(ch * SEQ, (ch + 1) * SEQ)
                for k, bank, free, ready in ((0, H1, s_si, s_h1), (1, H2, s_pr, None)):
                    if not (isinstance(n, int) and n < 2):
                        pe.wait_ge(free, n - 1)
                    last = products(pe, ps[:, bank + i, :],
                                    [(w[:, par, c, k, rows], f[:, c, toks])
                                     for w, f in ((w12h, fh), (w12l, fh), (w12h, fl)) for c in range(KC)])
                    if ready is not None:
                        last.then_inc(ready, 1)

            def weights(n, par, ch, i):
                if not (isinstance(n, int) and n < 2):
                    pe.wait_ge(s_hd, n - 1)
                pe.matmul(ps[:, HC + i, :], kind_s[:, par, i * P:(i + 1) * P], comb_t[:, ch * SEQ:(ch + 1) * SEQ],
                          start=True, stop=True).then_inc(s_h2, 1)

            pe.wait_ge(s_wb, 3)
            for i in range(2):
                hidden(i, 0, 0, i)
            pe.wait_ge(s_cp, 1)
            for b in range(BATCH):
                for t in range(b * TOK_TILES, (b + 1) * TOK_TILES):
                    i = t % TOK_TILES
                    ins = turned(pe, ps[0:PARTS, HC + b, i * P:(i + 1) * P], parts[:, t, :], ident[:, :])
                ins.then_inc(s_ct, 1)
            pe.wait_ge(s_ce, BATCH)
            for i in range(2):
                weights(i, 0, 0, i)

            def pairs(g, last):
                for op in ffn_steps(last):
                    if op[0] == "h":
                        q, i = op[1:]
                        if q % BATCH == 0 and i == 0:
                            pe.wait_ge(s_wb, 6 * g + 3 * (q // BATCH) + 3)
                        unit = (4 * BATCH * g + 2 * q + i, q // BATCH % 2, q % BATCH, i)
                        hidden(*unit)
                        weights(*unit)
                    elif op[0] == "y":
                        q, t = op[1:]
                        if t == 0:
                            pe.wait_ge(s_hl, 4 * BATCH * g + 2 * q + 2)
                        pe.wait_ge(s_yr, 8 * BATCH * g + 4 * q + t + 1)
                        toks = slice(t * P, (t + 1) * P)
                        products(pe, ps[:, HY + t % 2, :],
                                 [(a[:, q % 2, i, toks], w[:, q // BATCH, i, :])
                                  for i in range(2) for a, w in ((hh, w3h), (hh, w3l), (hl, w3h))]).then_inc(s_y, 1)

            over_pairs(pe, pairs)

        @block.scalar
        def _(act):
            act.nop().then_inc(s_exp, 1)
            act.nop().then_inc(s_te, 1)
            def high(t):
                act.wait_ge(s_xt, t + 1)
                act.copy(xh[:, :, t * P:(t + 1) * P],
                         ps[:, S_BANK + t % 4, :].rearrange("p (c n) -> p c n", c=KC)).then_inc(s_xh, 1)

            for t in range(TOK_TILES):
                high(t)

            def split_in(n):
                act.copy(wh[:, :, columns(n)], w_raw[:, :, columns(n)]).then_inc(s_wh, 1)

            def take(piece, b, bank):
                name = PROJ_ORDER[piece]
                src = ps[:, G_BANK + bank, :]
                if piece == 0:
                    ins = act.copy(k_t[:, b % 2, :], src)
                elif piece == 1:
                    ins = act.copy(v_t[:, :], src)
                else:
                    ins = act.mul(q_t[:, b % 2, name, :], src, ATT_SCALE)
                return ins

            def exponentials(g, u):
                w = (u % TOK_TILES + 1) * P
                act.wait_ge(s_max, N_UNIT * g + u + 1)
                act.activation(probs[:, u % 4, 0:w], ps[:, S_BANK + u % 2, 0:w], ACT.Exp,
                               bias=nmax[:, u % 4:u % 4 + 1], accum_out=rsum[:, u % 4:u % 4 + 1]).then_inc(s_exp, 1)

            act.wait_ge(s_w, 16)
            for n in range(NPROJ):
                split_in(n)
            for n, behind in PROLOGUE:
                act.wait_ge(s_g, n + 1)
                take(n, 0, n % 2).then_inc(s_q, 1)
                for t in behind:
                    high(t)
            act.wait_ge(s_t, 1)
            act.copy(v_s[:, 0, :, :], ps[:, T_BANK, :].rearrange("p (j d) -> p j d", j=TOK_TILES)).then_inc(s_te, 1)
            exponentials(0, 0)

            def take_turned(kind, which, slot, value):
                act.wait_ge({"k": s_kt, "q": s_qt, "m": s_mt}[kind], value)
                dst = {"k": k3[:, slot, which, :], "q": q3[:, slot % 2, which, :], "m": q3m[:, which, :]}[kind]
                act.copy(dst, ps[:, XT, :]).then_inc(s_ta, 1)

            def group(g, last):
                for op, c, t, k in walk(last):
                    if op[0] == "first_t":
                        take_turned(op[1], op[2], op[3], 2 * op[3] + op[2] + 1)
                    elif op[0] == "score":
                        exponentials(g, op[1])
                    elif op[0] == "split_out":
                        if op[1] == 0:
                            act.wait_ge(s_w, 32 * g + 32)
                            act.wait_ge(s_g, NPROJ + N_CHAIN * g)
                        act.copy(woh[:, op[1], :], wo_raw[:, op[1], :]).then_inc(s_wh, 1)
                    elif op[0] == "split_in":
                        if op[1] == 0:
                            act.wait_ge(s_w, 32 * g + 48)
                        split_in(op[1])
                    elif op[0] == "turn":
                        i = op[1] % TOK_TILES
                        act.wait_ge(s_t, N_TURN * g + t + 2)
                        act.copy(pt[:, 0:i + 1, i * P:(i + 1) * P],
                                 ps[:, T_BANK + (1 + t) % 2, 0:(i + 1) * P].rearrange("p (j n) -> p j n", n=P))\
                           .then_inc(s_te, 1)
                    elif op[0] == "pv":
                        act.wait_ge(s_pv, N_HEAD * g + op[1] + 1)
                        act.copy(ah[:, op[1] % QPG, :], ps[:, O_BANK + op[1] % 2, :]).then_inc(s_ah, 1)
                    elif op[0] == "chain" and is_chain(op):
                        act.wait_ge(s_g, NPROJ + N_CHAIN * g + c + 1)
                        take(piece_of(op[1]), op[2], c % 2).then_inc(s_q, 1)
                    elif op[0] == "chain":
                        act.wait_ge(s_t, N_TURN * g + t + 2)
                        act.copy(v_s[:, op[2] % 2, :, :],
                                 ps[:, T_BANK + (1 + t) % 2, :].rearrange("p (j d) -> p j d", j=TOK_TILES))\
                           .then_inc(s_te, 1)

            with act.Fori(0, GROUPS - 1) as g:
                group(g, False)
            group(GROUPS - 1, True)

            take_turned("m", 0, 0, 1)
            take_turned("q", 1, 1, 4)

            def cross(b, kv, steps):
                m = KV * b + kv
                for op in steps:
                    if op[0] == "st":
                        h, pair = op[1] // 2, op[1] % 2
                        act.wait_ge(s_st, 8 * m + op[1] + 1)
                        act.activation(xp[:, kv % 2, h, 2 * pair:2 * pair + 2, :],
                                       ps[:, XST + 2 * pair:XST + 2 * pair + 2, :], ACT.Exp,
                                       scale=X_SCALE).then_inc(s_xe, 1)
                    elif op[0] == "t" and op[1] != "o":
                        kind, which, off = op[1:]
                        take_turned(kind, which, (kv + off) % 4, 2 * (m + off) + which + 1)
                    elif op == ("pv", TOK_TILES - 1):
                        act.wait_ge(s_xpv, m)
                        act.copy(o_t[:, (kv - 1) % 2, :], ps[:, XO, :]).then_inc(s_oe, 1)

            over_items(cross)(act)

            act.wait_ge(s_gw, 16)
            act.copy(gate_s[:, :, 0:EXPERTS], gate_raw[:, :, :]).then_inc(s_gs, 1)
            for t in range(TILES):
                act.wait_ge(s_ft, t + 1)
                act.copy(fh[:, :, t * P:(t + 1) * P], ps[:, H1 + t % 2, :].rearrange("p (c n) -> p c n", c=KC))\
                   .then_inc(s_fh, 1)

            def split(par, n, value):
                if n < 2:
                    act.copy(w12h[:, par, :, n, :], w12_raw[:, :, n, :]).then_inc(s_wa, 1)
                else:
                    act.copy(kind_s[:, par, :], kind_raw[:, :]).then_inc(s_wa, 1)
                    act.copy(w3h[:, par, :, :], w3_raw[:, :, :]).then_inc(s_wa, 1)

            act.wait_ge(s_fw, 64)
            for n in range(3):
                split(0, n, n + 1)
            for b in range(BATCH):
                act.wait_ge(s_lg, b + 1)
                act.copy(by_expert[:, b * SEQ:(b + 1) * SEQ], ps[0:2 * EXPERTS, HC + b % 3, :]).then_inc(s_la, 1)
            act.wait_ge(s_lg, BATCH + 1)
            act.copy(glow[:, :, :], gate_ps[:, :, EXPERTS:]).then_inc(s_la, 1)
            act.wait_ge(s_lb, 1)
            act.activation(gprob[:, :, :], logit[:, :, :], ACT.Exp).then_inc(s_la, 1)
            def silu(n, i):
                act.wait_ge(s_h1, n + 1)
                act.activation(act_s[:, i, :], ps[:, H1 + i, :], ACT.Silu).then_inc(s_si, 1)

            def high(n, slot, i):
                act.wait_ge(s_hd, n + 1)
                act.copy(hh[:, slot, i, :], hid[:, i, :]).then_inc(s_hh, 1)

            for i in range(2):
                silu(i, i)
            for b in range(BATCH):
                act.wait_ge(s_ct, b + 1)
                act.copy(comb_t[:, b * SEQ:(b + 1) * SEQ], ps[0:PARTS, HC + b, :]).then_inc(s_ce, 1)
            for i in range(2):
                high(i, 0, i)

            def pairs(g, last):
                for op in ffn_steps(last):
                    if op[0] == "h":
                        n = 4 * BATCH * g + 2 * op[1] + op[2]
                        silu(n, op[2])
                        high(n, op[1] % 2, op[2])
                    elif op[0] == "w":
                        if op[2] == 0:
                            act.wait_ge(s_fw, 128 * g + 64 * op[1] + 128)
                        split(1 - op[1], op[2], None)

            over_pairs(act, pairs)

        @block.vector
        def _(dve):
            dve.nop().then_inc(s_res, 1)
            count = Count(s_dve)
            def low(t):
                dve.wait_ge(s_xh, t + 1)
                cols = slice(t * P, (t + 1) * P)
                dve.tensor_tensor(xl[:, :, cols], ps[:, S_BANK + t % 4, :].rearrange("p (c n) -> p c n", c=KC),
                                  xh[:, :, cols].bitcast(F32), ALU.subtract).then_inc(s_xl, 1)

            def moments_of(b):
                dve.wait_ge(s_x[b], 16)
                moments(dve, count, res[:, b * TOK_TILES:(b + 1) * TOK_TILES, :], norm, b * TOK_TILES, TOK_TILES, s_var)

            def roots_of(b):
                roots(dve, count, norm, b * TOK_TILES, TOK_TILES, s_pow, b + 1)

            def normal(dst, t):
                return dve.tensor_scalar(dst, res[:, t, :], mv[:, t, 0:1], rstd[:, t:t + 1], ALU.subtract, ALU.mult)

            def turnable(t):
                if t >= 4:
                    dve.wait_ge(s_xt, t - 3)
                normal(probs[:, t % 4, :], t).then_inc(s_xn, 1)

            def lows(b):
                for step in (turnable, low):
                    for t in range(b * TOK_TILES, (b + 1) * TOK_TILES):
                        step(t)

            def split(dst, hi, raw, value):
                dve.wait_ge(s_wh, value)
                dve.tensor_tensor(dst, raw, hi.bitcast(F32), ALU.subtract).then_inc(s_wl, 1)

            def split_in(n, value):
                split(wl[:, :, columns(n)], wh[:, :, columns(n)], w_raw[:, :, columns(n)], value)

            moments_of(0)
            roots_of(0)
            lows(0)
            for n in range(NPROJ):
                split_in(n, n + 1)
            moments_of(1)
            for b in range(1, BATCH):
                roots_of(b)
                if b < BATCH - 1:
                    moments_of(b + 1)
                lows(b)

            def maxima(g, u):
                w = (u % TOK_TILES + 1) * P
                dve.wait_ge(s_s, N_UNIT * g + u + 1)
                dve.tensor_reduce(nmax[:, u % 4:u % 4 + 1], ps[:, S_BANK + u % 2, 0:w], AX_X, ALU.max,
                                  negate=True).then_inc(s_max, 1)

            def weigh(g, u, count):
                i, w = u % 4, (u % TOK_TILES + 1) * P
                dve.wait_ge(s_exp, N_UNIT * g + u + 2)
                count.seal(dve, dve.reciprocal(rinv[:, i:i + 1], rsum[:, i:i + 1]))
                dve.tensor_scalar(probs[:, i, 0:w], probs[:, i, 0:w], rinv[:, i:i + 1], None, ALU.mult)\
                   .then_inc(s_pn, 1)

            maxima(0, 0)

            res_b = res[:, :, :].rearrange("p (b t) c -> p b t c", b=BATCH)

            def queries(b):
                for t in range(TOK_TILES):
                    dve.tensor_scalar(xn[:, t, :], res_b[:, b, t, :], mv[:, t, 0:1], rstd[:, t:t + 1],
                                      ALU.subtract, ALU.mult).then_inc(s_xn2, 1)

            def maximum(m, slot, u, bank):
                h, i = u // TOK_TILES, u % TOK_TILES
                dve.wait_ge(s_xs, 16 * m + u + 1)
                dve.tensor_reduce(xmax[:, slot, i, h:h + 1], ps[:, bank + u % 2, :], AX_X, ALU.max,
                                  negate=True).then_inc(s_xmax, 1)

            def group(g, last, base):
                count = Count(s_dve, base)
                weighed = 0
                for op, c, t, k in walk(last):
                    if op[0] == "moments":
                        dve.wait_ge(s_res, TILES * g + TOK_TILES + 1)
                        moments(dve, count, res_b[:, 0], norm, 0, TOK_TILES, s_var)
                    elif op[0] == "roots":
                        roots(dve, count, norm, 0, TOK_TILES, s_pow, BATCH + 1)
                    elif op[0] == "queries":
                        dve.wait_ge(s_q, N_QKV * GROUPS)
                        queries(0)
                    elif op[0] == "first_s":
                        maximum(0, 0, op[1], G_BANK)
                    if op[0] == "score":
                        maxima(g, op[1])
                    if op[0] == "score" or (op[0] == "turn" and op[1] >= weighed):
                        weigh(g, weighed, count)
                        weighed += 1
                    elif op[0] == "split_out":
                        split(wol[:, op[1], :], woh[:, op[1], :], wo_raw[:, op[1], :],
                              N_SPLIT * g + NPROJ + op[1] + 1)
                    elif op[0] == "split_in":
                        split_in(op[1], N_SPLIT * g + N_SPLIT + op[1] + 1)
                    elif op[0] == "pv":
                        dve.wait_ge(s_ah, N_HEAD * g + op[1] + 1)
                        dve.tensor_tensor(al[:, op[1] % QPG, :], ps[:, O_BANK + op[1] % 2, :],
                                          ah[:, op[1] % QPG, :].bitcast(F32), ALU.subtract).then_inc(s_al, 1)
                    elif op[0] == "out":
                        tile = op[2] * TOK_TILES + op[1]
                        dve.wait_ge(s_g, NPROJ + N_CHAIN * g + c + 1)
                        dve.tensor_tensor(res[:, tile, :], ps[:, G_BANK + c % 2, :], res[:, tile, :], ALU.add)\
                           .then_inc(s_res, 1)
                return count.n

            base = count.n
            with dve.Fori(0, GROUPS - 1) as g:
                used = group(g, False, N_UNIT * g + base)
            assert used == N_UNIT
            used = group(GROUPS - 1, True, N_UNIT * (GROUPS - 1) + base)

            count = Count(s_dve, N_UNIT * (GROUPS - 1) + base + used)
            counts = [count]

            def cross(b, kv, steps):
                m = KV * b + kv
                if kv == 0 and not (isinstance(b, int) and b in (0, BATCH)):
                    counts.append(Count(s_dve, counts[0].start + counts[0].n + X_MARKS * b - X_MARKS))
                count = counts[-1]
                if isinstance(b, int) and b == BATCH - 1:
                    if 4 <= kv < 7:
                        roots(dve, count, norm, (kv - 4) * TOK_TILES, TOK_TILES, s_pow, 2 * BATCH + kv - 3)
                    if 3 <= kv < 6:
                        moments(dve, count, res_b[:, kv - 3], norm, (kv - 3) * TOK_TILES, TOK_TILES, s_var)
                if not (isinstance(b, int) and b >= BATCH - 1):
                    if kv == 1:
                        moments(dve, count, res_b[:, b + 1], norm, 0, TOK_TILES, s_var)
                    if kv == 2:
                        roots(dve, count, norm, 0, TOK_TILES, s_pow, BATCH + 2 + b)
                    if kv == KV - 3:
                        dve.wait_ge(s_xq, KV * TOK_TILES * b + KV * TOK_TILES)
                        queries(b + 1)
                for op in steps:
                    if op[0] == "s":
                        maximum(m + 1, (kv + 1) % 2, op[1], XS)
                    elif op[:2] == ("t", "o"):
                        dve.wait_ge(s_ot, m - 1)
                        o = ps[:, XT, :].rearrange("p (t h d) -> p t h d", t=TOK_TILES, h=XG)
                        count.seal(dve, dve.reciprocal(xrec[:, :, :], o[:, :, :, XD]))
                        for t in range(TOK_TILES):
                            ready = count.mark(dve.tensor_tensor(
                                xo[:, t], o[:, t, :, 0:XD],
                                xrec[:, t, :].unsqueeze(2).to_broadcast([P, XG, XD]), ALU.mult))
                        dve.wait_ge(s_dve, ready)
                        at = ((kv - 2) % KV) * XG * XD
                        dst = res_b[:, b - (kv < 2), :, at:at + XG * XD]
                        dve.tensor_tensor(dst, xo[:, :, :, :].rearrange("p t h d -> p t (h d)"), dst, ALU.add)\
                            .then_inc(s_to, 1)

            over_items(cross)(dve)
            assert counts[1].n == X_MARKS

            dve.nop().then_inc(s_yr, 1)
            dve.nop().then_inc(s_yr, 1)
            count = counts[-1]
            dve.wait_ge(s_to, ITEMS)
            def low(t):
                dve.wait_ge(s_fh, t + 1)
                cols = slice(t * P, (t + 1) * P)
                dve.tensor_tensor(fl[:, :, cols], ps[:, H1 + t % 2, :].rearrange("p (c n) -> p c n", c=KC),
                                  fh[:, :, cols].bitcast(F32), ALU.subtract).then_inc(s_fl, 1)

            def turnable(t):
                if t >= 2:
                    dve.wait_ge(s_ft, t - 1)
                normal(fn[:, t % 2, :], t).then_inc(s_fn, 1)

            turnable(0)
            for t in range(TILES):
                if t + 1 < TILES:
                    turnable(t + 1)
                low(t)
                if t == 0:
                    dve.wait_ge(s_gs, 1)
                    dve.tensor_tensor(gate_s[:, :, EXPERTS:], gate_raw[:, :, :], gate_s[:, :, 0:EXPERTS].bitcast(F32),
                                      ALU.subtract).then_inc(s_gs, 1)
                if t == 1:
                    moments(dve, count, res_b[:, BATCH - 1], norm, TILES - TOK_TILES, TOK_TILES, s_var)
                if t == TOK_TILES + 1:
                    roots(dve, count, norm, TILES - TOK_TILES, TOK_TILES, s_pow, 3 * BATCH)

            def split(par, n, value):
                dve.wait_ge(s_wa, value)
                dst, hi, raw = ((w12l[:, par, :, n, :], w12h[:, par, :, n, :], w12_raw[:, :, n, :]) if n < 2 else
                                (w3l[:, par, :, :], w3h[:, par, :, :], w3_raw[:, :, :]))
                dve.tensor_tensor(dst, raw, hi.bitcast(F32), ALU.subtract).then_inc(s_wb, 1)

            for n in range(3):
                split(0, n, n + 1 + (n == 2))

            def spread(t):
                return t.unsqueeze(2).to_broadcast([P, TILES, EXPERTS])

            dve.wait_ge(s_la, BATCH + 1)
            count.seal(dve, dve.tensor_tensor(logit[:, :, :], gate_ps[:, :, 0:EXPERTS], glow[:, :, :], ALU.add))
            count.seal(dve, dve.tensor_reduce(gmax[:, :], logit[:, :, :], AX_X, ALU.max))
            dve.tensor_tensor(logit[:, :, :], logit[:, :, :], spread(gmax[:, :]), ALU.subtract).then_inc(s_lb, 1)
            dve.wait_ge(s_la, BATCH + 2)
            count.seal(dve, dve.tensor_reduce(gmax[:, :], gprob[:, :, :], AX_X, ALU.add))
            count.seal(dve, dve.reciprocal(gmax[:, :], gmax[:, :]))
            count.seal(dve, dve.tensor_tensor(gprob[:, :, :], gprob[:, :, :], spread(gmax[:, :]), ALU.mult))
            for t in range(TILES):
                ready = count.mark(dve.max(top[:, t, :], gprob[:, t, :]))
            dve.wait_ge(s_dve, ready)
            for t in range(TILES):
                ready = count.mark(dve.max_index(top_i[:, t, :], top[:, t, :], gprob[:, t, :]))
            dve.wait_ge(s_dve, ready)
            count.seal(dve, dve.tensor_copy(top_f[:, :, 0:2], top_i[:, :, 0:2]))
            numbers = number[:, :].unsqueeze(1).to_broadcast([P, TILES, EXPERTS])
            dve.wait_ge(s_cst, 8 + EXPERTS + 1)
            for n in range(2):
                ready = count.mark(dve.tensor_tensor(pick[:, n], numbers, spread(top_f[:, :, n]), ALU.is_equal))
            dve.wait_ge(s_dve, ready)
            count.seal(dve, dve.tensor_tensor(pick[:, 0], pick[:, 0], pick[:, 1], ALU.add))
            count.seal(dve, dve.tensor_tensor(comb[:, :, 0:EXPERTS], gprob[:, :, :], pick[:, 0], ALU.mult))
            count.seal(dve, dve.tensor_copy(comb_h[:, :, :], comb[:, :, :]))
            count.seal(dve, dve.tensor_copy(parts[:, :, 0:KINDS], comb_h[:, :, :]))
            count.seal(dve, dve.tensor_tensor(comb[:, :, :], comb[:, :, :], comb_h[:, :, :], ALU.subtract))
            count.seal(dve, dve.tensor_copy(comb_m[:, :, :], comb[:, :, :]))
            count.seal(dve, dve.tensor_copy(parts[:, :, KINDS:2 * KINDS], comb_m[:, :, :]))
            dve.tensor_tensor(parts[:, :, 2 * KINDS:], comb[:, :, :], comb_m[:, :, :], ALU.subtract).then_inc(s_cp, 1)

            def gated(n, i):
                dve.wait_ge(s_si, n + 1)
                dve.wait_ge(s_h2, n + 1)
                dve.tensor_tensor(prod[:, i, :], ps[:, H2 + i, :], act_s[:, i, :], ALU.mult).then_inc(s_pr, 1)
                dve.wait_ge(s_pr, n + 1)
                if not (isinstance(n, int) and n < 2):
                    dve.wait_ge(s_hl, n - 1)
                dve.tensor_tensor(hid[:, i, :], ps[:, HC + i, :], prod[:, i, :], ALU.mult).then_inc(s_hd, 1)

            gated(0, 0)
            gated(1, 1)

            def pairs(g, last):
                for op in ffn_steps(last):
                    if op[0] == "h":
                        gated(4 * BATCH * g + 2 * op[1] + op[2], op[2])
                    elif op[0] == "y":
                        q, t = op[1:]
                        tile = q % BATCH * TOK_TILES + t
                        dve.wait_ge(s_y, 8 * BATCH * g + 4 * q + t + 1)
                        dve.tensor_tensor(res[:, tile, :], ps[:, HY + t % 2, :], res[:, tile, :], ALU.add)\
                            .then_inc(s_yr, 1)
                    else:
                        split(1 - op[1], op[2], 8 * g + 4 * op[1] + 4 + op[2] + 1 + (op[2] == 2))

            over_pairs(dve, pairs)


def kernel(x, ctx_512, L0_attn_weight_qkv, L0_attn_weight_proj, L0_ffn_gate_w, L0_ffn_w1, L0_ffn_w2, L0_ffn_w3,
           L0_ffn_sw1, L0_ffn_sw2, L0_ffn_sw3):
    import numpy as np
    import concourse.bacc as bacc
    from concourse.bass_utils import run_bass_kernel_spmd

    f32 = np.float32

    def rows(experts, shared):
        experts = np.asarray(experts)
        n = experts.shape[0] * experts.shape[1]
        all_rows = np.zeros((ROWS_PAD, HID), f32)
        all_rows[:n] = experts.reshape(n, HID)
        all_rows[n:ROWS] = np.asarray(shared)
        return all_rows

    kinds = np.zeros((PARTS, ROWS_PAD), np.dtype("bfloat16"))
    for part in range(3):
        for e in range(KINDS):
            kinds[part * KINDS + e, e * WIDE:(e + 1) * WIDE if e < EXPERTS else ROWS] = 1
    arrays = {
        "x": np.ascontiguousarray(x),
        "ctx": np.ascontiguousarray(ctx_512),
        "w_qkv_t": np.ascontiguousarray(np.asarray(L0_attn_weight_qkv).T),
        "w_proj_t": np.ascontiguousarray(np.asarray(L0_attn_weight_proj).T),
        "gate_t": np.ascontiguousarray(np.asarray(L0_ffn_gate_w).T),
        "w1_t": np.ascontiguousarray(rows(L0_ffn_w1, L0_ffn_sw1).T),
        "w2_t": np.ascontiguousarray(rows(L0_ffn_w2, L0_ffn_sw2).T),
        "w3_t": rows(np.asarray(L0_ffn_w3).transpose(0, 2, 1), np.asarray(L0_ffn_sw3).T),
        "kinds": kinds,
    }
    nc = bacc.Bacc("TRN2", target_bir_lowering=False, num_devices=1)
    args = [nc.dram_tensor(f"in_{n}", a.shape, mybir.dt.from_np(a.dtype), kind="ExternalInput").ap()
            for n, a in arrays.items()]
    out = nc.dram_tensor("out", (BATCH, SEQ, HID), F32, kind="ExternalOutput").ap()
    build(nc, *args, out)
    r = run_bass_kernel_spmd(nc, [{f"in_{n}": a for n, a in arrays.items()}], core_ids=[0])
    return r.results[0]["out"]
```
